# Optimizing a Trainium2 kernel written in Bass

```python
import numpy as np
import jax
import jax.numpy as jnp

def _softmax(x, axis=-1):
    return jax.nn.softmax(x, axis=axis)

def _gelu(x):
    return jax.nn.gelu(x, approximate=True)

def _silu(x):
    return jax.nn.silu(x)

def _sigmoid(x):
    return jax.nn.sigmoid(x)

def _layernorm(x, axis=-1, eps=1e-05):
    m = jnp.mean(x, axis=axis, keepdims=True)
    v = jnp.var(x, axis=axis, keepdims=True)
    return (x - m) / jnp.sqrt(v + eps)

def _scatter_add(tgt, idx, src, axis=0):
    return tgt.at[idx].add(src)

def _segment_sum(src, seg, n):
    return jax.ops.segment_sum(src, seg, n)
kernel_name = 'mk_gnn_ffn_d1_gnn_r32_8b60ea'

def setup_inputs(seed: int=0):
    np.random.seed(seed)
    _w = jnp.asarray

    def _rec_inputs():
        import jax
        import jax.numpy as jnp
        _gk = jax.random.key(seed)
        x = -0.0003713 + 1 * jax.random.normal(jax.random.fold_in(_gk, 1), (3125, 256), jnp.float32)
        src = jax.random.randint(jax.random.fold_in(_gk, 2), (50000,), 0, 3125, jnp.int32)
        dst = jnp.minimum((3125 * jax.random.uniform(jax.random.fold_in(_gk, 3), (50000,)) ** 2.0).astype(jnp.int32), 99999)
        _o = jnp.argsort(dst, stable=True)
        src = src[_o]
        dst = dst[_o]
        edge_attr_3 = -1.09012e-05 + 0.99985 * jax.random.normal(jax.random.fold_in(_gk, 11), (50000, 3), jnp.float32)
        return (x, src, dst, edge_attr_3)
    x, src, dst, edge_attr_3 = _rec_inputs()

    def _L0_gnn_setup():
        import jax, jax.numpy as jnp
        import numpy as np
        N = 50000
        E = 12500
        IN = 256
        H = 8
        D = 32
        EF = 3
        key = jax.random.key(seed)
        ks = jax.random.split(key, 8)
        x = jax.random.normal(ks[0], (N, IN), dtype=jnp.float32)
        edge_index = jax.random.randint(ks[1], (2, E), 0, N, dtype=jnp.int64)
        edge_attr = jax.random.normal(ks[2], (E, EF), dtype=jnp.float32)
        W = jax.random.normal(ks[3], (H * D, IN), dtype=jnp.float32) * np.float32(np.sqrt(2.0 / (IN + H * D)))
        a_src = jax.random.normal(ks[4], (H, D), dtype=jnp.float32) * np.float32(np.sqrt(2.0 / (H + D)))
        a_dst = jax.random.normal(ks[5], (H, D), dtype=jnp.float32) * np.float32(np.sqrt(2.0 / (H + D)))
        edge_W = jax.random.normal(ks[6], (H * D, EF), dtype=jnp.float32) * np.float32(np.sqrt(2.0 / (EF + H * D)))
        edge_b = jnp.zeros((H * D,), dtype=jnp.float32)
        bias = jnp.zeros((H * D,), dtype=jnp.float32)
        return {'x': x, 'W': W, 'a_src': a_src, 'a_dst': a_dst, 'edge_W': edge_W, 'edge_b': edge_b, 'bias': bias, 'edge_attr': edge_attr, 'edge_index': edge_index}
    _L0_gnn_all = _L0_gnn_setup()
    _L0_gnn_in = {k: v for k, v in _L0_gnn_all.items() if k in ('W', 'a_src', 'a_dst', 'edge_W', 'edge_b', 'bias')}
    del _L0_gnn_all

    def _L0_ffn_setup():
        import jax, jax.numpy as jnp
        import numpy as np
        E, D, H, TOP_K = (6, 256, 256, 2)
        ROUTER_H = D // 2
        key = jax.random.key(seed)
        ks = jax.random.split(key, 12)
        s = 1.0 / np.sqrt(D)
        sh = 1.0 / np.sqrt(H)
        sr = 1.0 / np.sqrt(ROUTER_H)
        return {'features': jax.random.normal(ks[0], (8, 128, D), dtype=jnp.float32), 'router_w1': jax.random.uniform(ks[1], (D, ROUTER_H), jnp.float32, -s, s), 'router_b1': jnp.zeros((ROUTER_H,), jnp.float32), 'router_w2': jax.random.uniform(ks[2], (ROUTER_H, E), jnp.float32, -sr, sr), 'router_b2': jnp.zeros((E,), jnp.float32), 'expert_w1': jax.random.uniform(ks[3], (E, D, H), jnp.float32, -s, s), 'expert_b1': jnp.zeros((E, H), jnp.float32), 'expert_w2': jax.random.uniform(ks[4], (E, H, H), jnp.float32, -sh, sh), 'expert_b2': jnp.zeros((E, H), jnp.float32), 'expert_w3': jax.random.uniform(ks[5], (E, H, D), jnp.float32, -sh, sh), 'expert_b3': jnp.zeros((E, D), jnp.float32)}
    _L0_ffn_all = _L0_ffn_setup()
    _L0_ffn_in = {k: v for k, v in _L0_ffn_all.items() if k in ('router_w1', 'router_b1', 'router_w2', 'router_b2', 'expert_w1', 'expert_b1', 'expert_w2', 'expert_b2', 'expert_w3', 'expert_b3')}
    del _L0_ffn_all
    return {'x': x, 'src': src, 'dst': dst, 'edge_attr_3': edge_attr_3, 'L0_gnn_W': _L0_gnn_in['W'], 'L0_gnn_a_src': _L0_gnn_in['a_src'], 'L0_gnn_a_dst': _L0_gnn_in['a_dst'], 'L0_gnn_edge_W': _L0_gnn_in['edge_W'], 'L0_gnn_edge_b': _L0_gnn_in['edge_b'], 'L0_gnn_bias': _L0_gnn_in['bias'], 'L0_ffn_router_w1': _L0_ffn_in['router_w1'], 'L0_ffn_router_b1': _L0_ffn_in['router_b1'], 'L0_ffn_router_w2': _L0_ffn_in['router_w2'], 'L0_ffn_router_b2': _L0_ffn_in['router_b2'], 'L0_ffn_expert_w1': _L0_ffn_in['expert_w1'], 'L0_ffn_expert_b1': _L0_ffn_in['expert_b1'], 'L0_ffn_expert_w2': _L0_ffn_in['expert_w2'], 'L0_ffn_expert_b2': _L0_ffn_in['expert_b2'], 'L0_ffn_expert_w3': _L0_ffn_in['expert_w3'], 'L0_ffn_expert_b3': _L0_ffn_in['expert_b3']}

def reference(x, src, dst, edge_attr_3, L0_gnn_W, L0_gnn_a_src, L0_gnn_a_dst, L0_gnn_edge_W, L0_gnn_edge_b, L0_gnn_bias, L0_ffn_router_w1, L0_ffn_router_b1, L0_ffn_router_w2, L0_ffn_router_b2, L0_ffn_expert_w1, L0_ffn_expert_b1, L0_ffn_expert_w2, L0_ffn_expert_b2, L0_ffn_expert_w3, L0_ffn_expert_b3):
    import jax
    import jax.numpy as jnp

    def _L0_gnn_ref(x, W, a_src, a_dst, edge_W, edge_b, bias, edge_attr, edge_index):
        import jax, jax.numpy as jnp
        import numpy as np
        N = 50000
        E = 12500
        IN = 256
        H = 8
        D = 32
        EF = 3
        n = x.shape[0]
        h = (x @ W.T).reshape(n, H, D)
        src, dst = (edge_index[0], edge_index[1])
        h_src = h[src]
        h_dst = h[dst]
        alpha = jnp.einsum('ehd,hd->eh', h_src, a_src) + jnp.einsum('ehd,hd->eh', h_dst, a_dst)
        enc = jax.nn.relu(edge_attr @ edge_W.T + edge_b).reshape(-1, H, D)
        alpha = alpha + jnp.sum(enc * h_dst, axis=-1)
        alpha = jnp.where(alpha >= 0, alpha, 0.2 * alpha)
        amax = jax.ops.segment_max(alpha, dst, num_segments=n)
        ex = jnp.exp(alpha - amax[dst])
        denom = jax.ops.segment_sum(ex, dst, num_segments=n)
        attn = ex / jnp.maximum(denom[dst], 1e-10)
        out = jax.ops.segment_sum(h_src * attn[..., None], dst, num_segments=n)
        return out.reshape(n, H * D) + bias

    def _L0_ffn_ref(features, router_w1, router_b1, router_w2, router_b2, expert_w1, expert_b1, expert_w2, expert_b2, expert_w3, expert_b3):
        import jax, jax.numpy as jnp
        import numpy as np
        E, D, H, TOP_K = (6, 256, 256, 2)
        ROUTER_H = D // 2
        rh = jax.nn.relu(features @ router_w1 + router_b1)
        expert_logits = jax.nn.softmax(rh @ router_w2 + router_b2, axis=-1)
        top_w, top_i = jax.lax.top_k(expert_logits, TOP_K)
        routing_weights = jax.nn.softmax(top_w, axis=-1)
        h1 = jax.nn.relu(jnp.einsum('bsd,edh->bseh', features, expert_w1) + expert_b1)
        h2 = jax.nn.relu(jnp.einsum('bseh,ehf->bsef', h1, expert_w2) + expert_b2)
        expert_out = jnp.einsum('bsef,efo->bseo', h2, expert_w3) + expert_b3
        sel = jnp.take_along_axis(expert_out, top_i[:, :, :, None], axis=2)
        combined = jnp.sum(sel * routing_weights[..., None], axis=2)
        return combined
    edge_index = jnp.stack([src, dst])
    x = x + _L0_gnn_ref(_layernorm(x, axis=-1), L0_gnn_W, L0_gnn_a_src, L0_gnn_a_dst, L0_gnn_edge_W, L0_gnn_edge_b, L0_gnn_bias, edge_attr_3, edge_index)
    x = x + _L0_ffn_ref(_layernorm(x, axis=-1)[None], L0_ffn_router_w1, L0_ffn_router_b1, L0_ffn_router_w2, L0_ffn_router_b2, L0_ffn_expert_w1, L0_ffn_expert_b1, L0_ffn_expert_w2, L0_ffn_expert_b2, L0_ffn_expert_w3, L0_ffn_expert_b3)[0]
    return x

_drawn_inputs = setup_inputs


def setup_inputs(seed=0):
    import zlib

    import numpy as np

    out = dict(_drawn_inputs(seed))
    spreads = {'L0_gnn_edge_b': (0.0, 0.1),
     'L0_gnn_bias': (0.0, 0.1),
     'L0_ffn_router_b1': (0.0, 0.1),
     'L0_ffn_router_b2': (0.0, 0.1),
     'L0_ffn_expert_b1': (0.0, 0.756),
     'L0_ffn_expert_b2': (0.0, 0.32),
     'L0_ffn_expert_b3': (0.0, 0.1)}
    factors = {}
    for name, (base, spread) in spreads.items():
        noise = np.random.default_rng([zlib.crc32(name.encode()), seed]).standard_normal(out[name].shape)
        drawn = base * np.exp(spread * noise) if base else spread * noise
        out[name] = jnp.asarray(drawn.astype(out[name].dtype))
    for name, factor in factors.items():
        out[name] = (out[name] * factor).astype(out[name].dtype)
    return out
```

```python
from contextlib import ExitStack

import concourse.bass as bass
from concourse import mybir

ALU = mybir.AluOpType
ACT = mybir.ActivationFunctionType
AX = mybir.AxisListType
F32 = mybir.dt.float32
BF16 = mybir.dt.bfloat16
I32 = mybir.dt.int32
U32 = mybir.dt.uint32
ds = bass.ds

P = 128
NODES, C = 3125, 256
H, D = 8, 32
EDGES, EF = 50000, 3
NW = -(-NODES // P)
TAIL = NODES - (NW - 1) * P
EB = 256
NB = -(-EDGES // EB)
BC = NB // 2
NK = NB + NW - 1
NKP = 224
KC = NKP // 2
NSUB = 2 * NKP
CH = 16
G = NSUB // CH
SL = G * P
ROW = H + C
HALL = H + C + H
WSHIFT = 7
PAD_DST = 4095
BIG = 1e30
NE, RH = 6, 128
EPS = 1e-5
SPLIT_X = (0, 0, 0, 1, 1, 2)
SPLIT_W = (0, 1, 2, 0, 1, 0)
NPROD = len(SPLIT_X)
KE = NPROD * EF + NPROD
UN = 4
NI = NK // UN
assert NB == 2 * BC and NKP % 2 == 0 and NSUB == CH * G and NK % UN == 0 and NKP >= NK + 4


def bass_gnn_moe(nc, x, src, dst, edge_attr, gnn_W, a_src, a_dst, edge_W, edge_b, gnn_bias,
                 router_w1, router_b1, router_w2, router_b2, expert_w1, expert_b1, expert_w2,
                 expert_b2, expert_w3, expert_b3, out):
    ctx = ExitStack()
    with ctx:
        def sb(name, shape, dt=F32):
            return ctx.enter_context(nc.sbuf_tensor(name, shape, dt))

        def sem(name):
            return ctx.enter_context(nc.semaphore(name))

        def sems(name, n):
            return [sem(f"{name}{i}") for i in range(n)]

        node_tab = nc.dram_tensor("node_tab", (NW * P, ROW), F32).ap()
        row_log = nc.dram_tensor("row_log", (NK, P, 2 * ROW), F32).ap()
        ea_log = nc.dram_tensor("ea_log", (NPROD * EF, NKP, EB), BF16).ap()
        drel_log = nc.dram_tensor("drel_log", (NKP, EB), BF16).ap()

        bank = [ctx.enter_context(nc.psum_tensor(f"bank{i}", [P, 512], F32)) for i in range(8)]

        ident = sb("ident", [P, P])
        iota_free = sb("iota_free", [P, NKP])
        iota_part = sb("iota_part", [P, 1])
        block_no = sb("block_no", [BC, 2])
        block_no128 = sb("block_no128", [BC, 2])
        step_no128 = sb("step_no128", [KC, 2])
        head_mask = sb("head_mask", [P, 2, H])
        bias_b = sb("bias_b", [P, C])
        rb2_b = sb("rb2_b", [P, NE])
        rw1 = sb("rw1", [P, 2, RH])
        rb1 = sb("rb1", [P, 1])
        rw2 = sb("rw2", [P, NE])
        eb1 = sb("eb1", [P, NE, 2])
        eb2 = sb("eb2", [P, NE, 2])
        eb3 = sb("eb3", [NE, C])
        a_col = sb("a_col", [P, 2, 2])
        a_blk = sb("a_blk", [P, 2, 2, H])
        we = sb("we", [P, 2, EF + 1])
        we_bf = sb("we_bf", [P, 3, 2, EF + 1], BF16)
        we_res = sb("we_res", [P, 2, EF + 1])
        we_rows = sb("we_rows", [P, 2, KE])
        we_T = sb("we_T", [KE, C], BF16)
        w_all = sb("w_all", [P, 2, HALL])
        stats = sb("stats", [P, NW, 6])
        mean = sb("mean", [P, NW])
        rstd = sb("rstd", [P, NW])
        lt = sb("lt", [P, 3, NW])
        window_row = sb("window_row", [1, NKP], I32)
        window_f = sb("window_f", [P, NKP])
        drel_col = sb("drel_col", [P, NKP, 2])
        src_col = sb("src_col", [P, NKP, 2], I32)
        idx = sb("idx", [P, 2, 4], I32)

        xs = sb("xs", [P, NW, C])
        big = sb("big", [P, NW * 3 * ROW // 2])
        h_parts = big[:, :].bitcast(BF16).rearrange("p (w s c) -> p w s c", w=NW, s=3)
        acc = big[:, 0:NW * ROW].rearrange("p (w c) -> p w c", w=NW)
        xT_all = big[:, 0:2 * NW * P].rearrange("p (k n) -> p k n", k=2)
        alpha = sb("alpha", [P, NSUB, H])
        arena = sb("arena", [P, 4 * SL + 8])
        scan = [arena[:, i * SL + (8 if i > 1 else 0):(i + 1) * SL + (8 if i > 1 else 0)] for i in range(4)]
        resets = arena[:, SL:2 * SL + 1]

        def carve(start, shape, dt=F32):
            n = 1
            for s in shape[1:]:
                n *= s
            words = n if dt != BF16 else n // 2
            ap = arena[0:shape[0], start:start + words]
            if dt != F32:
                ap = ap.bitcast(dt)
            if len(shape) == 3:
                ap = ap.rearrange("p (a b) -> p a b", a=shape[1])
            if len(shape) == 4:
                ap = ap.rearrange("p (a b c) -> p a b c", a=shape[1], b=shape[2])
            return ap, start + words

        at = 0
        dst_i, at = carve(at, [BC, 2, EB], I32)
        src_i, at = carve(at, [BC, 2, EB], I32)
        prev_i, at = carve(at, [BC, 2], I32)
        ea_f, at = carve(at, [BC, 2, EB * EF])
        dst_f, at = carve(at, [BC, 2, EB])
        src_f, at = carve(at, [BC, 2, EB])
        last_w, at = carve(at, [BC, 2], I32)
        prev_w, at = carve(at, [BC, 2], I32)
        last_k, at = carve(at, [BC, 2])
        prev_k, at = carve(at, [BC, 2])
        sel_a, at = carve(at, [BC, 2, NKP])
        sel, at = carve(at, [BC, 2, NKP])
        drel_bf, at = carve(at, [KC, 2, EB], BF16)
        ea_r, at = carve(at, [KC, 2, EF, EB])
        ea_bf, at = carve(at, [KC, 2 * 3 * EF, EB], BF16)
        w_nat, at = carve(at, [P, 2, C])
        assert at <= 4 * SL
        ew, at = carve(0, [P, 3 * NE, 2, C])
        assert at <= 4 * SL

        gath = sb("gath", [P, UN, 2, ROW])
        drel_b = sb("drel_b", [P, 2, 2, EB], BF16)
        ea_T = sb("ea_T", [KE, 2, 2, EB], BF16)
        hotT = sb("hotT", [P, UN, EB], BF16)
        renc = sb("renc", [P, 2, 2, EB])
        prod = sb("prod", [P, 2, 2, EB])
        hot = prod
        xn = sb("xn", [P, 2, C])
        xT = sb("xT", [P, 2, 2, P])
        hf = sb("hf", [P, 2, HALL])
        hr = sb("hr", [P, ROW])
        msg = sb("msg", [P, 2, 2, ROW])
        rh = sb("rh", [P, 2, P])
        hT1 = gath[:, :, :, :].rearrange("p a b c -> p (a b c)")[:, 0:4 * 512].rearrange("p (a b c) -> p a b c", a=2, b=2)
        hT2 = sb("hT2", [P, 2, 512])
        ends = sb("ends", [P, 4])
        erow = sb("erow", [1, 4, P])
        dlink = sb("dlink", [1, 6, P])
        valid = sb("valid", [P, NSUB])
        mask_add = sb("mask_add", [P, NSUB])
        key = sb("key", [P, NSUB])
        carry = sb("carry", [1, 2, P])
        carry_c = sb("carry_c", [P, 2])
        rden = sb("rden", [P, NW, H])
        lg = sb("lg", [P, NW, H])
        rsm = sb("rsm", [P, 6, NW])
        top = sb("top", [P, NW, 8])
        topi = sb("topi", [P, NW, 8], U32)
        topf = sb("topf", [P, NW, 2])
        wts = sb("wts", [P, NW, H])
        wt2 = sb("wt2", [P, NW, H])
        wt_ring = sb("wt_ring", [P, 2, H])
        wT = sb("wT", [H, 2, P])

        s_const = sem("s_const")
        s_pad = sem("s_pad")
        s_edges = sem("s_edges")
        s_x = sem("s_x")
        s_wt = sem("s_wt")
        s_wt2 = sem("s_wt2")
        s_ew = sem("s_ew")
        s_dve = sem("s_dve")
        s_wps = sem("s_wps")
        s_wsb = sem("s_wsb")
        s_ablk = sem("s_ablk")
        s_we = sem("s_we")
        s_sel = sem("s_sel")
        s_selps = sem("s_selps")
        s_src = sem("s_src")
        s_logsrc = sem("s_logsrc")
        s_logs = sem("s_logs")
        s_var = sem("s_var")
        s_std = sem("s_std")
        s_bn = sem("s_bn")
        s_xn = sem("s_xn")
        s_xnT = sem("s_xnT")
        s_xT = sem("s_xT")
        s_hps = sem("s_hps")
        s_hf = sem("s_hf")
        s_split = sem("s_split")
        s_tab = sems("s_tab", 2)
        s_idx = sem("s_idx")
        s_g = sems("s_g", UN)
        s_log = sems("s_log", UN)
        s_drel = sems("s_drel", 2)
        s_ea = sems("s_ea", 2)
        s_hot = sem("s_hot")
        s_hd = sem("s_hd")
        s_enc = sem("s_enc")
        s_relu = sem("s_relu")
        s_prod = sem("s_prod")
        s_pal = sem("s_pal")
        s_al = sem("s_al")
        s_perm = sem("s_perm")
        s_tp = sem("s_tp")
        s_tc = sem("s_tc")
        s_ends = sem("s_ends")
        s_row = sem("s_row")
        s_carry = sem("s_carry")
        s_dif = sem("s_dif")
        s_exp = sem("s_exp")
        s_bp = sem("s_bp")
        s_bc = sem("s_bc")
        s_ld = sems("s_ld", UN)
        s_oh = sem("s_oh")
        s_msg = sem("s_msg")
        s_exc = sem("s_exc")
        s_agg = sem("s_agg")
        s_acc = sem("s_acc")
        s_xn2 = sem("s_xn2")
        s_t2 = sem("s_t2")
        s_xT2 = sem("s_xT2")
        s_rps = sem("s_rps")
        s_rh = sem("s_rh")
        s_lps = sem("s_lps")
        s_lg = sem("s_lg")
        s_soft = sem("s_soft")
        s_softe = sem("s_softe")
        s_wr = sem("s_wr")
        s_wtps = sem("s_wtps")
        s_wtT = sem("s_wtT")
        s_b3 = sem("s_b3")
        s_b3a = sem("s_b3a")
        s_l1 = sem("s_l1")
        s_h1 = sem("s_h1")
        s_l2 = sem("s_l2")
        s_h2 = sem("s_h2")
        s_l3 = sem("s_l3")
        s_l3t = sem("s_l3t")
        s_y = sem("s_y")
        s_out = sem("s_out")
        s_gate_act, s_gate_pe, s_gate_pool, s_gate_dve = (sem(f"s_gate_{n}") for n in ("act", "pe", "pool", "dve"))

        def flat(ap):
            return ap.rearrange("p a c -> p (a c)")

        def first(i):
            return isinstance(i, int) and i == 0

        def windows(eng, body):
            body(0, 0)
            body(0, 1)
            with eng.Fori(1, NW // 2) as i:
                body(i, 0)
                body(i, 1)
            body(NW // 2, 0)

        block = ctx.enter_context(nc.Block())

        @block.sync
        def _(sp):
            sp.wait_ge(s_pad, 5)
            full = (NB - 1) * EB
            for t, v in ((dst_i, dst), (src_i, src)):
                sp.dma_start(t[:, 0, :], v[0:BC * EB].rearrange("(p e) -> p e", p=BC)).then_inc(s_edges, 16)
                sp.dma_start(t[0:BC - 1, 1, :], v[BC * EB:full].rearrange("(p e) -> p e", p=BC - 1)).then_inc(s_edges, 16)
                sp.dma_start(t[BC - 1:BC, 1, 0:EDGES - full], v[full:EDGES].rearrange("(a e) -> a e", a=1)).then_inc(s_edges, 16)
            whole = dst[0:full].rearrange("(t e) -> t e", e=EB)
            with nc.allow_non_contiguous_dma("one word per block"):
                sp.dma_start(prev_i[1:BC, 0:1], whole[0:BC - 1, EB - 1:EB]).then_inc(s_edges, 16)
                sp.dma_start(prev_i[0:BC, 1:2], whole[BC - 1:NB - 1, EB - 1:EB]).then_inc(s_edges, 16)
            ev = edge_attr.rearrange("e c -> (e c)")
            EL = EB * EF
            sp.dma_start(ea_f[:, 0, :], ev[0:BC * EL].rearrange("(p e) -> p e", p=BC)).then_inc(s_edges, 16)
            sp.dma_start(ea_f[0:BC - 1, 1, :], ev[BC * EL:(NB - 1) * EL].rearrange("(p e) -> p e", p=BC - 1)).then_inc(s_edges, 16)
            sp.dma_start(ea_f[BC - 1:BC, 1, 0:EDGES * EF - (NB - 1) * EL],
                         ev[(NB - 1) * EL:EDGES * EF].rearrange("(a e) -> a e", a=1)).then_inc(s_edges, 16)
            sp.dma_start(xs[:, 0:NW - 1, :], x[0:(NW - 1) * P, :].rearrange("(w p) c -> p w c", p=P)).then_inc(s_x, 16)
            sp.dma_start(xs[0:TAIL, NW - 1, :], x[(NW - 1) * P:NODES, :]).then_inc(s_x, 16)

            sp.wait_ge(s_logsrc, 1)
            for kb in range(2):
                sp.dma_start(drel_log[kb * KC:(kb + 1) * KC, :], drel_bf[:, kb, :]).then_inc(s_logs, 16)
                for q in range(NPROD):
                    a = kb * 9 + SPLIT_X[q] * EF
                    sp.dma_start(ea_log[q * EF:(q + 1) * EF, kb * KC:(kb + 1) * KC, :].rearrange("c k e -> k c e"),
                                 ea_bf[:, a:a + EF, :]).then_inc(s_logs, 16)

            def table(i, slot):
                w = 2 * i + slot
                sp.wait_ge(s_hf, w + 3)
                sp.dma_start(node_tab[ds(w * P, P), :], hf[:, slot, 0:ROW]).then_inc(s_tab[slot], 16)
            windows(sp, table)

            sp.wait_ge(s_logs, 16 * 2 * (1 + NPROD))

            def load_pair(i, p):
                k = UN * i + 2 * p
                if not first(i):
                    sp.wait_ge(s_hot, k)
                    sp.wait_ge(s_enc, k)
                sp.dma_start(drel_b[:, p, :, :], drel_log[ds(k, 2), :].partition_broadcast(P)).then_inc(s_drel[p], 16)
                sp.dma_start(ea_T[0:NPROD * EF, p, :, :], ea_log[:, ds(k, 2), :]).then_inc(s_ea[p], 16)

            load_pair(0, 0)
            load_pair(0, 1)
            with sp.Fori(0, NI) as i:
                load_pair(i + 1, 0)
                load_pair(i + 1, 1)
                for u in range(UN):
                    sp.wait_ge(s_g[u], 32 * i + 32)
                    sp.dma_start(row_log[ds(UN * i + u, 1), :, :].rearrange("k p c -> p (k c)"),
                                 gath[:, u, :, :].rearrange("p a c -> p (a c)")).then_inc(s_log[u], 16)
            for p in range(2):
                sp.wait_ge(s_drel[p], 16 * (NI + 1))
                sp.wait_ge(s_ea[p], 16 * (NI + 1))
            for u in range(UN):
                sp.wait_ge(s_log[u], 16 * NI)
            sp.wait_ge(s_al, UN + NK)
            with sp.Fori(0, NI) as i:
                for u in range(UN):
                    sp.wait_ge(s_msg, UN * i + u + 1)
                    sp.dma_start(gath[:, u, :, :].rearrange("p a c -> p (a c)"),
                                 row_log[ds(UN * i + u, 1), :, :].rearrange("k p c -> p (k c)")).then_inc(s_ld[u], 16)
            sp.wait_ge(s_y, 1 + NW * NE)
            sp.dma_start(out[0:(NW - 1) * P, :].rearrange("(w p) c -> p w c", p=P), xs[:, 0:NW - 1, :]).then_inc(s_out, 16)
            sp.dma_start(out[(NW - 1) * P:NODES, :], xs[0:TAIL, NW - 1, :]).then_inc(s_out, 16)
            sp.wait_ge(s_out, 32)

        @block.gpsimd
        def _(pool):
            pool.memset(dst_i, PAD_DST).then_inc(s_pad, 1)
            pool.memset(src_i, 0).then_inc(s_pad, 1)
            pool.memset(prev_i, 0).then_inc(s_pad, 1)
            pool.memset(ea_f, 0.0).then_inc(s_pad, 1)
            pool.memset(xs[:, NW - 1, :], 0.0).then_inc(s_pad, 1)
            pool.memset(ident[:, :], 0.0).then_inc(s_const, 1)
            for t, pattern, mul in ((iota_free, [[1, NKP]], 0), (iota_part, [[0, 1]], 1), (block_no, [[BC, 2]], 1),
                                    (block_no128, [[BC * P, 2]], P), (step_no128, [[KC * P, 2]], P)):
                pool.iota(t[:, :], pattern, 0, mul, allow_small_or_imprecise_dtypes=True).then_inc(s_const, 1)
            pool.memset(head_mask[:, :, :], 0.0).then_inc(s_const, 1)
            pool.memset(ea_T[:, :, :, :], 1.0).then_inc(s_const, 1)
            pool.wait_ge(s_const, 8)
            pool.affine_select(out=ident[:, :], in_=ident[:, :], compare_op=ALU.not_equal, fill=1.0,
                               base=0, pattern=[[-1, P]], channel_multiplier=1).then_inc(s_const, 1)

            pool.wait_ge(s_tab[0], 16 * ((NW + 1) // 2))
            pool.wait_ge(s_tab[1], 16 * (NW // 2))
            pool.wait_ge(s_src, 1)

            def gather(i):
                for p in range(2):
                    pool.wait_ge(s_al, UN * i + 2 * p + 2)
                    pool.sem_inc(s_gate_pool, 1)
                    pool.tensor_copy(idx[:, p, :], src_col[:, ds(UN * i + 2 * p, 2), :].rearrange("p a b -> p (a b)")).then_inc(s_idx, 1)
                    pool.wait_ge(s_idx, 2 * i + p + 1)
                    for u in (2 * p, 2 * p + 1):
                        if not first(i):
                            pool.wait_ge(s_log[u], 16 * i)
                        pool.sem_inc(s_gate_pool, 1)
                        for j in range(2):
                            c = 2 * (u % 2) + j
                            pool.indirect_dma_start(
                                out=gath[:, u, j, :], out_offset=None, in_=node_tab[:, :],
                                in_offset=bass.IndirectOffsetOnAxis(ap=idx[:, p, c:c + 1], axis=0)).then_inc(s_g[u], 16)
            gather(0)
            with pool.Fori(1, NI) as i:
                gather(i)

        @block.scalar
        def _(act):
            for s, depth in ((s_xT, 2), (s_hf, 2), (s_relu, 2), (s_xT2, 2), (s_rh, 2), (s_wtT, 2), (s_h1, 1), (s_h2, 1)):
                act.sem_inc(s, depth)
            act.dma_start(w_nat, gnn_W.rearrange("(a p) k -> p a k", p=P)).then_inc(s_wt, 16)
            with nc.allow_non_contiguous_dma("small weight columns"):
                act.dma_start(a_col[:, :, 0], a_src.rearrange("h d -> (h d)").rearrange("(a p) -> p a", p=P)).then_inc(s_wt, 16)
                act.dma_start(a_col[:, :, 1], a_dst.rearrange("h d -> (h d)").rearrange("(a p) -> p a", p=P)).then_inc(s_wt, 16)
                act.dma_start(we[:, :, 0:EF], edge_W.rearrange("(a p) c -> p a c", p=P)).then_inc(s_wt, 16)
                act.dma_start(we[:, :, EF], edge_b.rearrange("(a p) -> p a", p=P)).then_inc(s_wt, 16)
                act.dma_start(rb1[:, :], router_b1.rearrange("(p a) -> p a", a=1)).then_inc(s_wt2, 16)
                for e in range(NE):
                    act.dma_start(eb1[:, e, :], expert_b1[e, :].rearrange("(a p) -> p a", p=P)).then_inc(s_wt2, 16)
                    act.dma_start(eb2[:, e, :], expert_b2[e, :].rearrange("(a p) -> p a", p=P)).then_inc(s_wt2, 16)
            act.dma_start(bias_b[:, :], gnn_bias.partition_broadcast(P)).then_inc(s_wt2, 16)
            act.dma_start(rb2_b[:, :], router_b2.partition_broadcast(P)).then_inc(s_wt2, 16)
            act.dma_start(rw1[:, :, :], router_w1.rearrange("(a p) f -> p a f", p=P)).then_inc(s_wt2, 16)
            act.dma_start(rw2[:, :], router_w2).then_inc(s_wt2, 16)
            act.dma_start(eb3[:, :], expert_b3).then_inc(s_wt2, 16)

            act.wait_ge(s_wps, 1)
            act.activation(w_all[:, :, H:H + C], bank[7][:, :].rearrange("p (k c) -> p k c", k=2), ACT.Copy).then_inc(s_wsb, 1)
            act.wait_ge(s_wps, 2)
            pa = bank[6][:, 0:32].rearrange("p (k s h) -> p k s h", k=2, s=2)
            act.activation(w_all[:, :, 0:H], pa[:, :, 0, :], ACT.Copy).then_inc(s_wsb, 1)
            act.activation(w_all[:, :, H + C:HALL], pa[:, :, 1, :], ACT.Copy).then_inc(s_wsb, 1)
            act.wait_ge(s_wps, 3)
            act.activation(we_T[:, :], bank[5][0:KE, 0:C], ACT.Copy).then_inc(s_wsb, 1)

            act.wait_ge(s_var, 1)
            act.activation(rstd[:, :], lt[:, 0, :], ACT.Sqrt).then_inc(s_std, 1)

            def project(i, slot):
                w = 2 * i + slot
                act.wait_ge(s_xnT, w + 3)
                act.wait_ge(s_hps, w + 1)
                act.sem_inc(s_gate_act, 1)
                act.activation(xT[:, slot, :, :], bank[slot][:, 0:C].rearrange("p (k n) -> p k n", k=2), ACT.Copy).then_inc(s_xT, 1)
                act.wait_ge(s_hps, w + 3)
                if not first(i):
                    act.wait_ge(s_tab[slot], 16 * i)
                act.wait_ge(s_split, 4 * w + 2)
                act.sem_inc(s_gate_act, 1)
                act.activation(hf[:, slot, :], bank[2 + slot][:, 0:HALL], ACT.Copy).then_inc(s_hf, 1)
            windows(act, project)

            def relu(k, v):
                act.wait_ge(s_enc, k + 3)
                act.wait_ge(s_prod, k + 1)
                act.sem_inc(s_gate_act, 1)
                act.activation(renc[:, v, :, :], bank[2 + v][:, :].rearrange("p (a e) -> p a e", a=2), ACT.Relu).then_inc(s_relu, 1)
            relu(0, 0)
            with act.Fori(0, NI) as i:
                for u in range(UN):
                    relu(UN * i + u + 1, (u + 1) % 2)

            act.wait_ge(s_perm, 1)
            for n in range(2 * G):
                act.wait_ge(s_tp, n + 1)
                act.activation(scan[2 + n // G][:, n % G * P:(n % G + 1) * P], bank[n % 8][:, 0:P], ACT.Copy).then_inc(s_tc, 1)
            act.wait_ge(s_dif, 1)
            act.activation(scan[0], scan[2], ACT.Exp).then_inc(s_exp, 1)
            view = alpha[:, :, :].rearrange("p (j g) h -> p g j h", j=CH)
            for g in range(G):
                act.wait_ge(s_bp, g + 1)
                act.activation(view[:, g, :, :], bank[g % 8][:, 0:P].rearrange("p (j h) -> p j h", j=CH), ACT.Copy).then_inc(s_bc, 1)
            act.wait_ge(s_bp, G)
            for n, w in enumerate((expert_w1, expert_w2, expert_w3)):
                for e in range(NE):
                    act.dma_start(ew[:, n * NE + e, :, :], w[e].rearrange("(a p) f -> p a f", p=P)).then_inc(s_ew, 16)

            act.wait_ge(s_bc, G)
            with act.Fori(0, NK // 2) as i:
                for v in range(2):
                    k = 2 * i + v
                    act.wait_ge(s_agg, k + 1)
                    act.sem_inc(s_gate_act, 1)
                    act.activation(msg[:, v, :, 0:H], alpha[:, ds(2 * k, 2), :], ACT.Copy).then_inc(s_exc, 1)

            act.wait_ge(s_var, 2)
            act.activation(rstd[:, :], lt[:, 0, :], ACT.Sqrt).then_inc(s_std, 1)
            act.wait_ge(s_wt2, 16 * (1 + 2 * NE + 5))

            def route(i, slot):
                w = 2 * i + slot
                act.wait_ge(s_t2, w + 3)
                act.sem_inc(s_gate_act, 1)
                act.activation(xT_all[:, :, ds(w * P, P)], bank[slot][:, 0:C].rearrange("p (k n) -> p k n", k=2), ACT.Copy).then_inc(s_xT2, 1)
                act.wait_ge(s_rps, w + 1)
                act.wait_ge(s_lps, w + 1)
                act.sem_inc(s_gate_act, 1)
                act.activation(rh[:, slot, :], bank[2 + slot][:, 0:P], ACT.Relu, bias=rb1[:, 0:1]).then_inc(s_rh, 1)
            windows(act, route)

            act.wait_ge(s_soft, 1)
            act.activation(lg[:, :, 0:NE], lg[:, :, 0:NE], ACT.Exp).then_inc(s_softe, 1)
            act.wait_ge(s_soft, 2)
            act.activation(rsm[:, 2, :], rsm[:, 1, :], ACT.Exp).then_inc(s_softe, 1)

            def turn_weights(i, slot):
                w = 2 * i + slot
                act.wait_ge(s_wtps, w + 3)
                act.wait_ge(s_b3, w + 1)
                act.sem_inc(s_gate_act, 1)
                act.activation(wT[:, slot, :], bank[slot][0:H, 0:P], ACT.Copy).then_inc(s_wtT, 1)
            windows(act, turn_weights)

            def experts(g, n):
                def layer1(e):
                    c = NE * g + e
                    act.wait_ge(s_l1, c + 1)
                    act.wait_ge(s_l2, c + 1)
                    act.sem_inc(s_gate_act, 1)
                    for m in range(2):
                        a = act.activation(hT1[:, e % 2, m, 0:n], bank[m][:, 0:n], ACT.Relu, bias=eb1[:, e, m:m + 1])
                    a.then_inc(s_h1, 1)
                layer1(0)
                for e in range(NE):
                    c = NE * g + e
                    act.wait_ge(s_l2, c + 3)
                    act.wait_ge(s_l3, c + 1)
                    act.sem_inc(s_gate_act, 1)
                    for m in range(2):
                        a = act.activation(hT2[:, m, 0:n], bank[2 + m][:, 0:n], ACT.Relu, bias=eb2[:, e, m:m + 1])
                    a.then_inc(s_h2, 1)
                    if e + 1 < NE:
                        layer1(e + 1)
            with act.Fori(0, NW // 4) as g:
                experts(g, 4 * P)
            experts(NW // 4, NW % 4 * P)

        @block.tensor
        def _(pe):
            mm = pe.matmul
            for s, depth in ((s_xnT, 2), (s_hps, 2), (s_enc, 2), (s_pal, 4), (s_agg, 2), (s_t2, 2), (s_lps, 2),
                             (s_wtps, 2), (s_b3, 2), (s_l2, 2), (s_l3, 1)):
                pe.sem_inc(s, depth)
            pe.wait_ge(s_const, 9)
            pe.wait_ge(s_wt, 80)
            for kb in range(2):
                for ob in range(2):
                    t = pe.transpose(bank[7][:, kb * C + ob * P:kb * C + (ob + 1) * P], w_nat[:, ob, kb * P:(kb + 1) * P], ident[:, :])
            t.then_inc(s_wps, 1)
            pe.wait_ge(s_ablk, 1)
            for kb in range(2):
                for ob in range(2):
                    t = mm(bank[6][:, kb * 16:kb * 16 + 16], w_nat[:, ob, kb * P:(kb + 1) * P],
                           a_blk[:, ob, :, :].rearrange("p a h -> p (a h)"), start=ob == 0, stop=ob == 1)
            t.then_inc(s_wps, 1)
            pe.wait_ge(s_we, 1)
            for ob in range(2):
                t = pe.transpose(bank[5][0:KE, ob * P:(ob + 1) * P], we_rows[:, ob, :], ident[:, :])
            t.then_inc(s_wps, 1)

            pe.wait_ge(s_sel, 1)
            pe.wait_ge(s_wsb, 4)
            for a in range(2):
                t = mm(bank[0][:, 0:NKP], block_no[:, a:a + 1].broadcast_to([BC, P]), sel[:, a, :], start=a == 0, stop=a == 1)
            t.then_inc(s_selps, 1)
            for j in range(2):
                for a in range(2):
                    t = mm(bank[3][:, j * NKP:(j + 1) * NKP], src_f[:, a, j * P:(j + 1) * P], sel[:, a, :], start=a == 0, stop=a == 1)
            t.then_inc(s_selps, 1)
            for j in range(2):
                for a in range(2):
                    t = mm(bank[2][:, j * NKP:(j + 1) * NKP], dst_f[:, a, j * P:(j + 1) * P], sel[:, a, :], start=a == 0, stop=a == 1)
            t.then_inc(s_selps, 1)
            for kb in range(2):
                for a in range(2):
                    t = mm(bank[1][0:KC, kb * EB:(kb + 1) * EB], sel[:, a, kb * KC:(kb + 1) * KC], dst_f[:, a, :], start=a == 0, stop=a == 1)
            t.then_inc(s_selps, 1)
            for c in range(EF):
                for kb in range(2):
                    for a in range(2):
                        t = mm(bank[4 + c][0:KC, kb * EB:(kb + 1) * EB], sel[:, a, kb * KC:(kb + 1) * KC],
                               ea_f[:, a, :].rearrange("p (e c) -> p c e", c=EF)[:, c, :], start=a == 0, stop=a == 1)
                t.then_inc(s_selps, 1)
            pe.wait_ge(s_logsrc, 1)

            def project(i, slot):
                w = 2 * i + slot
                pe.wait_ge(s_xn, w + 1)
                pe.wait_ge(s_xT, w + 1)
                pe.sem_inc(s_gate_pe, 1)
                for kb in range(2):
                    t = pe.transpose(bank[slot][:, kb * P:(kb + 1) * P], xn[:, slot, kb * P:(kb + 1) * P], ident[:, :])
                t.then_inc(s_xnT, 1)
                pe.wait_ge(s_xT, w + 3)
                pe.wait_ge(s_hf, w + 1)
                pe.sem_inc(s_gate_pe, 1)
                for kb in range(2):
                    t = mm(bank[2 + slot][:, 0:HALL], xT[:, slot, kb, :], w_all[:, kb, :], start=kb == 0, stop=kb == 1)
                t.then_inc(s_hps, 1)
            windows(pe, project)

            pe.wait_ge(s_xT, 2 + NW)
            pe.wait_ge(s_hf, 2 + NW)
            pe.wait_ge(s_split, 8 + 4 * NW)

            def look_up(k, u, kp, w):
                v = u % 2
                pe.wait_ge(s_ea[u // 2], 16 * kp + 16)
                pe.wait_ge(s_relu, k + 1)
                pe.sem_inc(s_gate_pe, 1)
                for half in range(2):
                    t = mm(bank[2 + v][:, half * EB:(half + 1) * EB], we_T[:, half * P:(half + 1) * P],
                           ea_T[:, u // 2, v, :], start=True, stop=True)
                t.then_inc(s_enc, 1)
                pe.wait_ge(s_hot, k + 3)
                pe.wait_ge(s_prod, k + 1)
                pe.sem_inc(s_gate_pe, 1)
                for half in range(2):
                    for s in range(3):
                        t = mm(bank[v][:, half * EB:(half + 1) * EB],
                               h_parts[:, ds(w, 1), s, half * P:(half + 1) * P].rearrange("p a c -> p (a c)"),
                               hotT[:, u, :], start=s == 0, stop=s == 2)
                t.then_inc(s_hd, 1)

            def logits(k, u, w):
                v = u % 2
                pe.wait_ge(s_prod, k + 3)
                pe.wait_ge(s_al, k + 3)
                pe.sem_inc(s_gate_pe, 1)
                for j in range(2):
                    o = bank[4 + v][:, j * H:(j + 1) * H]
                    for half in range(2):
                        mm(o, prod[:, v, half, j * P:(j + 1) * P], head_mask[:, half, :], start=half == 0, stop=False)
                    for s in range(3):
                        t = mm(o, hotT[:, u, j * P:(j + 1) * P],
                               h_parts[:, ds(w, 1), s, C:C + H].rearrange("p a c -> p (a c)"), start=False, stop=s == 2)
                t.then_inc(s_pal, 1)

            def window_of(k):
                return pe.value_load(window_row[0:1, ds(k, 1)], min_val=0, max_val=NW - 1)

            look_up(0, 0, 0, window_of(0))
            with pe.Fori(0, NI) as i:
                k0 = UN * i
                w = window_of(k0)
                for u in range(UN):
                    wn = window_of(k0 + (u + 1))
                    look_up(k0 + (u + 1), (u + 1) % UN, i + (u + 1) // UN, wn)
                    logits(k0 + u, u, w)
                    w = wn

            pe.wait_ge(s_perm, 1)
            pe.wait_ge(s_relu, 2 + NK + 1)
            for n in range(2 * G):
                if n >= 8:
                    pe.wait_ge(s_tc, n - 7)
                pe.transpose(bank[n % 8][:, 0:P], scan[n // G][:, n % G * P:(n % G + 1) * P], ident[:, :]).then_inc(s_tp, 1)
            pe.wait_ge(s_ends, 1)
            for c in range(4):
                t = pe.transpose(bank[0][0:1, c * P:(c + 1) * P], ends[:, c:c + 1], ident[:, :])
            t.then_inc(s_row, 1)
            pe.wait_ge(s_carry, 1)
            for c in range(2):
                t = pe.transpose(bank[1][:, c:c + 1], carry[0:1, c, :], ident[0:1, 0:1])
            t.then_inc(s_row, 1)
            pe.wait_ge(s_exp, 1)
            for g in range(G):
                if g >= 8:
                    pe.wait_ge(s_bc, g - 7)
                pe.transpose(bank[g % 8][:, 0:P], scan[0][:, g * P:(g + 1) * P], ident[:, :]).then_inc(s_bp, 1)

            pe.wait_ge(s_bc, G)
            with pe.Fori(0, NK // 2) as i:
                for v in range(2):
                    k = 2 * i + v
                    pe.wait_ge(s_oh, k + 1)
                    pe.wait_ge(s_msg, k + 5)
                    pe.wait_ge(s_exc, k + 1)
                    pe.wait_ge(s_acc, k + 1)
                    pe.sem_inc(s_gate_pe, 1)
                    for j in range(2):
                        t = mm(bank[v][:, 0:ROW], hot[:, v, j, 0:P], msg[:, v, j, :], start=j == 0, stop=j == 1)
                    t.then_inc(s_agg, 1)

            pe.wait_ge(s_acc, 2 + NK)
            pe.wait_ge(s_wt2, 16 * (1 + 2 * NE + 5))

            def route(i, slot):
                w = 2 * i + slot
                pe.wait_ge(s_xn2, w + 1)
                pe.wait_ge(s_xT2, w + 1)
                pe.sem_inc(s_gate_pe, 1)
                for kb in range(2):
                    t = pe.transpose(bank[slot][:, kb * P:(kb + 1) * P], xn[:, slot, kb * P:(kb + 1) * P], ident[:, :])
                t.then_inc(s_t2, 1)
                pe.wait_ge(s_xT2, w + 3)
                pe.wait_ge(s_rh, w + 1)
                pe.sem_inc(s_gate_pe, 1)
                for kb in range(2):
                    t = mm(bank[2 + slot][:, 0:P], rw1[:, kb, :], xT_all[:, kb, ds(w * P, P)], start=kb == 0, stop=kb == 1)
                t.then_inc(s_rps, 1)
                pe.wait_ge(s_rh, w + 3)
                pe.wait_ge(s_lg, w + 1)
                pe.sem_inc(s_gate_pe, 1)
                mm(bank[4 + slot][:, 0:NE], rh[:, slot, :], rw2[:, :], start=True, stop=True).then_inc(s_lps, 1)
            windows(pe, route)

            def biases(i, slot):
                w = 2 * i + slot
                pe.wait_ge(s_wr, w + 1)
                pe.wait_ge(s_wtT, w + 1)
                pe.sem_inc(s_gate_pe, 1)
                pe.transpose(bank[slot][0:H, 0:P], wt_ring[:, slot, :], ident[:, :]).then_inc(s_wtps, 1)
                pe.wait_ge(s_wtT, w + 3)
                pe.wait_ge(s_b3a, w + 1)
                pe.sem_inc(s_gate_pe, 1)
                mm(bank[2 + slot][:, 0:C], wT[0:NE, slot, :], eb3[:, :], start=True, stop=True).then_inc(s_b3, 1)
            windows(pe, biases)

            pe.wait_ge(s_wtT, 2 + NW)
            pe.wait_ge(s_b3a, 2 + NW)
            pe.wait_ge(s_ew, 16 * 3 * NE)

            def experts(g, tiles):
                n = tiles * P

                def layer1(e):
                    pe.wait_ge(s_h1, NE * g + e + 1)
                    pe.sem_inc(s_gate_pe, 1)
                    for m in range(2):
                        for kb in range(2):
                            t = mm(bank[m][:, 0:n], ew[:, e, kb, m * P:(m + 1) * P], xT_all[:, kb, ds(g * 4 * P, n)],
                                   start=kb == 0, stop=kb == 1)
                    t.then_inc(s_l1, 1)
                layer1(0)
                for e in range(NE):
                    c = NE * g + e
                    pe.wait_ge(s_h1, c + 2)
                    pe.wait_ge(s_h2, c + 1)
                    pe.sem_inc(s_gate_pe, 1)
                    for m in range(2):
                        for kb in range(2):
                            t = mm(bank[2 + m][:, 0:n], ew[:, NE + e, kb, m * P:(m + 1) * P], hT1[:, e % 2, kb, 0:n],
                                   start=kb == 0, stop=kb == 1)
                    t.then_inc(s_l2, 1)
                    if e + 1 < NE:
                        layer1(e + 1)
                    pe.wait_ge(s_h2, c + 2)
                    pe.sem_inc(s_gate_pe, 1)
                    for q in range(tiles):
                        pe.wait_ge(s_y, 4 * NE * g + ((e - 1) * tiles + q + 2 if e else 1))
                        pe.sem_inc(s_gate_pe, 1)
                        for kb in range(2):
                            t = mm(bank[4 + q][:, 0:C], hT2[:, kb, q * P:(q + 1) * P], ew[:, 2 * NE + e, kb, :],
                                   start=kb == 0, stop=kb == 1)
                        t.then_inc(s_l3t, 1)
                    pe.wait_ge(s_l3t, 4 * NE * g + (e + 1) * tiles)
                    pe.sem_inc(s_l3, 1)
            with pe.Fori(0, NW // 4) as g:
                experts(g, 4)
            experts(NW // 4, NW % 4)

        @block.vector
        def _(dve):
            done = [0]

            def link(ins):
                done[0] += 1
                ins.then_inc(s_dve, 1)
                dve.wait_ge(s_dve, done[0])
                return ins

            for s, depth in ((s_hot, 2), (s_prod, 2), (s_al, UN), (s_split, 8), (s_msg, UN), (s_acc, 2), (s_lg, 2), (s_b3a, 2), (s_y, 1)):
                dve.sem_inc(s, depth)
            link(dve.memset(alpha[:, 2 * NK:NSUB, :], 0.0))
            link(dve.memset(lg[:, :, NE:H], -1.0))
            link(dve.memset(we_rows[:, :, :], 0.0))

            dve.wait_ge(s_const, 9)
            dve.wait_ge(s_wt, 80)
            for q in range(4):
                for half in range(2):
                    c = 4 * half + q
                    link(dve.memset(head_mask[q * D:(q + 1) * D, half, c:c + 1], 1.0))
            for ob in range(2):
                for s in range(2):
                    t = link(dve.tensor_scalar(a_blk[:, ob, s, :], head_mask[:, ob, :], a_col[:, ob, s:s + 1], None, ALU.mult))
            dve.sem_inc(s_ablk, 1)
            link(dve.tensor_copy(we_bf[:, 0, :, :], we[:, :, :]))
            link(dve.tensor_tensor(we_res[:, :, :], we[:, :, :], we_bf[:, 0, :, :], ALU.subtract))
            link(dve.tensor_copy(we_bf[:, 1, :, :], we_res[:, :, :]))
            link(dve.tensor_tensor(we_bf[:, 2, :, :], we_res[:, :, :], we_bf[:, 1, :, :], ALU.subtract))
            for q in range(NPROD):
                link(dve.tensor_copy(we_rows[:, :, q * EF:(q + 1) * EF], we_bf[:, SPLIT_W[q], :, 0:EF]))
            for q in range(3):
                link(dve.tensor_copy(we_rows[:, :, NPROD * EF + q:NPROD * EF + q + 1], we_bf[:, q, :, EF:EF + 1]))
            dve.sem_inc(s_we, 1)

            dve.wait_ge(s_edges, 16 * 11)
            link(dve.tensor_scalar(last_w, dst_i[:, :, EB - 1], WSHIFT, None, ALU.logical_shift_right))
            link(dve.tensor_scalar(prev_w, prev_i, WSHIFT, None, ALU.logical_shift_right))
            link(dve.tensor_tensor(last_k, last_w, block_no[:, :], ALU.add))
            link(dve.tensor_tensor(prev_k, prev_w, block_no[:, :], ALU.add))
            link(dve.tensor_scalar(prev_k, prev_k, -1.0, None, ALU.add))
            for a in range(2):
                link(dve.tensor_scalar(sel_a[:, a, :], iota_free[0:BC, :], prev_k[:, a:a + 1], None, ALU.is_gt))
                link(dve.scalar_tensor_tensor(sel[:, a, :], iota_free[0:BC, :], last_k[:, a:a + 1], sel_a[:, a, :], ALU.is_le, ALU.mult))
                link(dve.tensor_copy(dst_f[:, a, :], dst_i[:, a, :]))
                link(dve.tensor_scalar(dst_f[:, a, :], dst_f[:, a, :], block_no128[:, a:a + 1], None, ALU.add))
                link(dve.tensor_copy(src_f[:, a, :], src_i[:, a, :]))
            dve.sem_inc(s_sel, 1)

            dve.wait_ge(s_selps, 1)
            link(dve.tensor_tensor(window_f[:, :], iota_free[:, :], bank[0][:, 0:NKP], ALU.subtract))
            link(dve.tensor_scalar(window_row[:, :], window_f[0:1, :], float(NW - 1), None, ALU.min))
            dve.wait_ge(s_selps, 2)
            link(dve.tensor_copy(src_col[:, :, :].rearrange("p k j -> p j k"), bank[3][:, 0:2 * NKP].rearrange("p (j k) -> p j k", j=2)))
            dve.sem_inc(s_src, 1)
            dve.wait_ge(s_selps, 3)
            link(dve.scalar_tensor_tensor(drel_col[:, :, :].rearrange("p k j -> p j k"),
                                          iota_free[:, :].unsqueeze(1).broadcast_to([P, 2, NKP]), -float(P),
                                          bank[2][:, 0:2 * NKP].rearrange("p (j k) -> p j k", j=2), ALU.mult, ALU.add))
            dve.wait_ge(s_selps, 4)
            for kb in range(2):
                link(dve.tensor_scalar(drel_bf[:, kb, :], bank[1][0:KC, kb * EB:(kb + 1) * EB], step_no128[:, kb:kb + 1], None, ALU.subtract))
            dve.wait_ge(s_selps, 7)
            for c in range(EF):
                link(dve.tensor_copy(ea_r[:, :, c, :], bank[4 + c][0:KC, :].rearrange("p (k e) -> p k e", k=2)))
            for kb in range(2):
                hi, mid, lo = (ea_bf[:, kb * 9 + s * EF:kb * 9 + (s + 1) * EF, :] for s in range(3))
                link(dve.tensor_copy(hi, ea_r[:, kb, :, :]))
                link(dve.tensor_tensor(ea_r[:, kb, :, :], ea_r[:, kb, :, :], hi, ALU.subtract))
                link(dve.tensor_copy(mid, ea_r[:, kb, :, :]))
                link(dve.tensor_tensor(lo, ea_r[:, kb, :, :], mid, ALU.subtract))
            dve.sem_inc(s_logsrc, 1)

            def norm_stats(n):
                with dve.Fori(0, NW) as w:
                    dve.bn_stats(flat(stats[:, ds(w, 1), :]), flat(xs[:, ds(w, 1), :])).then_inc(s_bn, 1)
                dve.wait_ge(s_bn, NW * n)
                link(dve.tensor_tensor(mean[:, :], stats[:, :, 1], stats[:, :, 4], ALU.add))
                link(dve.tensor_scalar(mean[:, :], mean[:, :], 0.5, None, ALU.mult))
                link(dve.tensor_tensor(lt[:, 1, :], stats[:, :, 1], stats[:, :, 4], ALU.subtract))
                link(dve.tensor_tensor(lt[:, 1, :], lt[:, 1, :], lt[:, 1, :], ALU.mult))
                link(dve.tensor_tensor(lt[:, 2, :], stats[:, :, 2], stats[:, :, 5], ALU.add))
                link(dve.tensor_scalar(lt[:, 2, :], lt[:, 2, :], 1.0 / C, EPS, ALU.mult, ALU.add))
                link(dve.scalar_tensor_tensor(lt[:, 0, :], lt[:, 1, :], 0.25, lt[:, 2, :], ALU.mult, ALU.add))
                dve.sem_inc(s_var, 1)
                dve.wait_ge(s_std, n)
                link(dve.reciprocal(rstd[:, :], rstd[:, :]))

            def normalise(w, slot, freed, made):
                dve.wait_ge(freed, w + 1)
                dve.tensor_scalar(xn[:, slot, :], flat(xs[:, ds(w, 1), :]), mean[:, ds(w, 1)], rstd[:, ds(w, 1)],
                                  ALU.subtract, ALU.mult).then_inc(made, 1)

            dve.wait_ge(s_x, 32)
            dve.wait_ge(s_pad, 5)
            norm_stats(1)
            normalise(0, 0, s_xnT, s_xn)

            def split(i, slot):
                w = 2 * i + slot
                if not (isinstance(w, int) and w == NW - 1):
                    normalise(w + 1, 1 - slot, s_xnT, s_xn)
                dve.wait_ge(s_hf, w + 3)
                dve.sem_inc(s_gate_dve, 1)
                hi, mid, lo = (h_parts[:, ds(w, 1), s, :].rearrange("p a c -> p (a c)") for s in range(3))
                dve.tensor_copy(hi, hf[:, slot, H:HALL]).then_inc(s_split, 1)
                dve.wait_ge(s_split, 4 * w + 9)
                dve.tensor_tensor(hr[:, :], hf[:, slot, H:HALL], hi, ALU.subtract).then_inc(s_split, 1)
                dve.wait_ge(s_split, 4 * w + 10)
                dve.sem_inc(s_gate_dve, 1)
                dve.tensor_copy(mid, hr[:, :]).then_inc(s_split, 1)
                dve.wait_ge(s_split, 4 * w + 11)
                dve.tensor_tensor(lo, hr[:, :], mid, ALU.subtract).then_inc(s_split, 1)
            windows(dve, split)

            def one_hot(k, u, kp):
                dve.wait_ge(s_drel[u // 2], 16 * kp + 16)
                dve.wait_ge(s_pal, k + 1)
                dve.tensor_scalar(hotT[:, u, :], drel_b[:, u // 2, u % 2, :], iota_part[:, 0:1], None, ALU.is_equal).then_inc(s_hot, 1)

            def products(k, v):
                dve.wait_ge(s_relu, k + 3)
                dve.wait_ge(s_hd, k + 1)
                dve.wait_ge(s_pal, k + 3)
                dve.tensor_tensor(prod[:, v, :, :], renc[:, v, :, :], bank[v][:, :].rearrange("p (a e) -> p a e", a=2), ALU.mult).then_inc(s_prod, 1)

            def complete(k, u, kg):
                dve.wait_ge(s_pal, k + 5)
                dve.wait_ge(s_g[u], 32 * kg)
                dve.tensor_tensor(alpha[:, ds(2 * k, 2), :], bank[4 + u % 2][:, 0:2 * H].rearrange("p (j h) -> p j h", j=2),
                                  gath[:, u, :, 0:H], ALU.add).then_inc(s_al, 1)

            def first_phase(i, peeled=False):
                for u in range(UN):
                    k = UN * i + u
                    products(k, u % 2)
                    one_hot(k + 2, (u + 2) % UN, i + (u + 2) // UN)
                    if not (peeled and u == 0):
                        complete(k - 1, (u - 1) % UN, i + 1 if u else i)
            one_hot(0, 0, 0)
            one_hot(1, 1, 0)
            first_phase(0, peeled=True)
            with dve.Fori(1, NI) as i:
                first_phase(i)
            complete(NK - 1, UN - 1, NI)

            dve.wait_ge(s_al, UN + NK)
            flat_drel = drel_col[:, :, :].rearrange("p k j -> p (k j)")
            link(dve.tensor_scalar(key[:, :], flat_drel, 0.0, None, ALU.is_ge))
            link(dve.scalar_tensor_tensor(valid[:, :], flat_drel, float(P - 1), key[:, :], ALU.is_le, ALU.mult))
            link(dve.tensor_scalar(mask_add[:, :], valid[:, :], BIG, -BIG, ALU.mult, ALU.add))
            link(dve.scalar_tensor_tensor(key[:, :].rearrange("p (k j) -> p k j", j=2),
                                          window_f[:, :].unsqueeze(2).broadcast_to([P, NKP, 2]), float(P),
                                          drel_col[:, :, :], ALU.mult, ALU.add))
            link(dve.scalar_tensor_tensor(key[:, :], key[:, :], 1.0, valid[:, :], ALU.add, ALU.mult))
            link(dve.tensor_scalar(key[:, :], key[:, :], -1.0, None, ALU.add))
            link(dve.scalar_tensor_tensor(alpha[:, :, :], alpha[:, :, :], 0.2, alpha[:, :, :], ALU.mult, ALU.max))
            perm = "p (g j h) -> p g j h"
            link(dve.tensor_tensor(scan[0].rearrange(perm, g=G, j=CH), alpha[:, :, :].rearrange("p (j g) h -> p g j h", j=CH),
                                   mask_add[:, :].rearrange("p (j g) -> p g j", j=CH).unsqueeze(3).broadcast_to([P, G, CH, H]), ALU.add))
            link(dve.tensor_copy(scan[1].rearrange(perm, g=G, j=CH),
                                 key[:, :].rearrange("p (j g) -> p g j", j=CH).unsqueeze(3).broadcast_to([P, G, CH, H])))
            dve.sem_inc(s_perm, 1)

            dve.wait_ge(s_tc, 2 * G)
            logit_T, key_T = scan[2], scan[3]
            link(dve.tensor_tensor(resets[:, 1:SL], key_T[:, 1:SL], key_T[:, 0:SL - 1], ALU.not_equal))
            link(dve.memset(resets[:, 0:1], 0.0))
            link(dve.memset(resets[:, SL:SL + 1], 0.0))
            link(dve.tensor_scalar(resets, resets, -BIG, None, ALU.mult))
            link(dve.tensor_copy(ends[:, 2:3], key_T[:, 0:1]))
            link(dve.tensor_copy(ends[:, 3:4], key_T[:, SL - 1:SL]))
            link(dve.tensor_tensor_scan(scan[0], resets[:, 0:SL], logit_T, -BIG, ALU.add, ALU.max))
            link(dve.tensor_tensor_scan(scan[3][:, ::-1], resets[:, 1:SL + 1][:, ::-1], scan[0][:, ::-1], -BIG, ALU.add, ALU.max))
            link(dve.tensor_copy(ends[:, 0:1], scan[0][:, SL - 1:SL]))
            link(dve.tensor_copy(ends[:, 1:2], scan[3][:, 0:1]))
            dve.sem_inc(s_ends, 1)

            dve.wait_ge(s_row, 1)
            link(dve.tensor_copy(erow[:, :, :].rearrange("p a n -> p (a n)"), bank[0][0:1, :]))
            last_max, first_max, first_key, last_key = (erow[:, c, :] for c in range(4))
            broken, cut, step_f, run_f, step_b, run_b = (dlink[:, c, :] for c in range(6))
            N1 = P - H
            link(dve.tensor_tensor(broken, first_key, last_key, ALU.not_equal))
            link(dve.tensor_scalar(broken, broken, -BIG, None, ALU.mult))
            link(dve.memset(cut, 1.0))
            link(dve.tensor_tensor(cut[:, H:P], first_key[:, H:P], last_key[:, 0:N1], ALU.not_equal))
            link(dve.tensor_scalar(cut, cut, -BIG, None, ALU.mult))
            link(dve.tensor_tensor(step_f, cut, broken, ALU.add))
            link(dve.memset(step_b, -BIG))
            link(dve.tensor_tensor(step_b[:, 0:N1], cut[:, H:P], broken[:, 0:N1], ALU.add))
            by_head = "p (j h) -> p h j"
            for h in range(H):
                f = [t.rearrange(by_head, h=H)[:, h, :] for t in (run_f, step_f, last_max)]
                b = [t.rearrange(by_head, h=H)[:, h, ::-1] for t in (run_b, step_b, first_max)]
                link(dve.tensor_tensor_scan(f[0], f[1], f[2], -BIG, ALU.add, ALU.max))
                link(dve.tensor_tensor_scan(b[0], b[1], b[2], -BIG, ALU.add, ALU.max))
            link(dve.memset(carry[:, :, :], -BIG))
            link(dve.tensor_tensor(carry[:, 0, H:P], run_f[:, 0:N1], cut[:, H:P], ALU.add))
            link(dve.tensor_tensor(carry[:, 1, 0:N1], run_b[:, H:P], cut[:, H:P], ALU.add))
            dve.sem_inc(s_carry, 1)
            dve.wait_ge(s_row, 2)
            link(dve.tensor_copy(carry_c[:, :], bank[1][:, 0:2]))
            link(dve.tensor_tensor_scan(scan[0], resets[:, 0:SL], logit_T, carry_c[:, 0:1], ALU.add, ALU.max))
            link(dve.tensor_tensor_scan(scan[3][:, ::-1], resets[:, 1:SL + 1][:, ::-1], scan[0][:, ::-1], carry_c[:, 1:2], ALU.add, ALU.max))
            link(dve.tensor_tensor(logit_T, logit_T, scan[3], ALU.subtract))
            dve.sem_inc(s_dif, 1)

            dve.wait_ge(s_hd, NK + 1)
            dve.wait_ge(s_pal, 4 + NK)
            link(dve.memset(acc, 0.0))
            dve.wait_ge(s_bc, G)

            def weigh(k, u, i):
                dve.wait_ge(s_ld[u], 16 * i + 16)
                dve.wait_ge(s_agg, k + 1)
                dve.tensor_tensor(msg[:, u % 2, :, H:ROW].rearrange("p j (h d) -> p j h d", h=H),
                                  gath[:, u, :, H:ROW].rearrange("p j (h d) -> p j h d", h=H),
                                  alpha[:, ds(2 * k, 2), :].unsqueeze(3).broadcast_to([P, 2, H, D]), ALU.mult).then_inc(s_msg, 1)

            def spread(k, v):
                dve.wait_ge(s_agg, k + 1)
                dve.tensor_tensor(hot[:, v, :, 0:P], iota_free[:, 0:P].unsqueeze(1).broadcast_to([P, 2, P]),
                                  flat(drel_col[:, ds(k, 1), :]).unsqueeze(2).broadcast_to([P, 2, P]),
                                  ALU.is_equal).then_inc(s_oh, 1)

            def add_up(k, v):
                w = dve.value_load(window_row[0:1, ds(k, 1)], min_val=0, max_val=NW - 1)
                dve.wait_ge(s_agg, k + 3)
                dve.wait_ge(s_acc, k + 2)
                a = flat(acc[:, ds(w, 1), :])
                dve.tensor_tensor(a, a, bank[v][:, 0:ROW], ALU.add).then_inc(s_acc, 1)

            def second_phase(i, peeled=False):
                for u in range(UN):
                    k = UN * i + u
                    spread(k, u % 2)
                    weigh(k, u, i)
                    if not (peeled and u == 0):
                        add_up(k - 1, (u - 1) % 2)
            second_phase(0, peeled=True)
            with dve.Fori(1, NI) as i:
                second_phase(i)
            add_up(NK - 1, 1)

            dve.wait_ge(s_acc, 2 + NK)
            dve.wait_ge(s_wt2, 16 * (1 + 2 * NE + 5))
            link(dve.tensor_scalar(rden[:, :, :], acc[:, :, 0:H], 1e-10, None, ALU.max))
            link(dve.reciprocal(rden[:, :, :], rden[:, :, :]))
            av = acc[:, :, H:ROW].rearrange("p w (h d) -> p w h d", h=H)
            link(dve.tensor_tensor(av, av, rden[:, :, :].unsqueeze(3).broadcast_to([P, NW, H, D]), ALU.mult))
            link(dve.tensor_tensor(acc[:, :, H:ROW], acc[:, :, H:ROW], bias_b[:, :].unsqueeze(1).broadcast_to([P, NW, C]), ALU.add))
            link(dve.tensor_tensor(xs[:, :, :], xs[:, :, :], acc[:, :, H:ROW], ALU.add))
            norm_stats(2)
            normalise(0, 0, s_t2, s_xn2)

            def route(i, slot):
                w = 2 * i + slot
                if not (isinstance(w, int) and w == NW - 1):
                    normalise(w + 1, 1 - slot, s_t2, s_xn2)
                dve.wait_ge(s_lps, w + 3)
                dve.tensor_tensor(flat(lg[:, ds(w, 1), 0:NE]), bank[4 + slot][:, 0:NE], rb2_b[:, :], ALU.add).then_inc(s_lg, 1)
            windows(dve, route)

            dve.wait_ge(s_lg, 2 + NW)

            def over(ap, n):
                return ap.unsqueeze(2).broadcast_to([P, NW, n])
            link(dve.tensor_reduce(rsm[:, 0, :], lg[:, :, 0:NE], AX.X, ALU.max))
            link(dve.tensor_tensor(lg[:, :, 0:NE], lg[:, :, 0:NE], over(rsm[:, 0, :], NE), ALU.subtract))
            dve.sem_inc(s_soft, 1)
            dve.wait_ge(s_softe, 1)
            link(dve.tensor_reduce(rsm[:, 0, :], lg[:, :, 0:NE], AX.X, ALU.add))
            link(dve.reciprocal(rsm[:, 0, :], rsm[:, 0, :]))
            link(dve.tensor_tensor(lg[:, :, 0:NE], lg[:, :, 0:NE], over(rsm[:, 0, :], NE), ALU.mult))
            for w in range(NW):
                link(dve.max(top[:, w, :], lg[:, w, :]))
                link(dve.max_index(topi[:, w, :], top[:, w, :], lg[:, w, :]))
            link(dve.tensor_tensor(rsm[:, 1, :], top[:, :, 1], top[:, :, 0], ALU.subtract))
            dve.sem_inc(s_soft, 1)
            link(dve.tensor_copy(topf[:, :, :], topi[:, :, 0:2]))
            dve.wait_ge(s_softe, 2)
            link(dve.tensor_scalar(rsm[:, 3, :], rsm[:, 2, :], 1.0, None, ALU.add))
            link(dve.reciprocal(rsm[:, 3, :], rsm[:, 3, :]))
            link(dve.tensor_tensor(rsm[:, 4, :], rsm[:, 2, :], rsm[:, 3, :], ALU.mult))
            nos = iota_free[:, 0:H].unsqueeze(1).broadcast_to([P, NW, H])
            for t, q in ((wts, 0), (wt2, 1)):
                link(dve.tensor_tensor(t[:, :, :], nos, over(topf[:, :, q], H), ALU.is_equal))
                link(dve.tensor_tensor(t[:, :, :], t[:, :, :], over(rsm[:, 3 + q, :], H), ALU.mult))
            link(dve.tensor_tensor(wts[:, :, :], wts[:, :, :], wt2[:, :, :], ALU.add))

            def stage(w, slot):
                dve.wait_ge(s_wtps, w + 1)
                dve.sem_inc(s_gate_dve, 1)
                dve.tensor_copy(wt_ring[:, slot, :], flat(wts[:, ds(w, 1), :])).then_inc(s_wr, 1)
            stage(0, 0)

            def add_biases(i, slot):
                w = 2 * i + slot
                if not (isinstance(w, int) and w == NW - 1):
                    stage(w + 1, 1 - slot)
                dve.wait_ge(s_b3, w + 3)
                a = flat(xs[:, ds(w, 1), :])
                dve.tensor_tensor(a, a, bank[2 + slot][:, 0:C], ALU.add).then_inc(s_b3a, 1)
            windows(dve, add_biases)
            dve.wait_ge(s_b3a, 2 + NW)

            def experts(g, tiles):
                for e in range(NE):
                    for q in range(tiles):
                        c = 4 * NE * g + e * tiles + q
                        dve.wait_ge(s_l3t, c + 1)
                        if e:
                            dve.wait_ge(s_y, c + 2 - tiles)
                        w = 4 * g + q
                        a = flat(xs[:, ds(w, 1), :])
                        dve.scalar_tensor_tensor(a, bank[4 + q][:, 0:C], flat(wts[:, ds(w, 1), e:e + 1]), a, ALU.mult, ALU.add).then_inc(s_y, 1)
            with dve.Fori(0, NW // 4) as g:
                experts(g, 4)
            experts(NW // 4, NW % 4)


_INS = ["x", "src", "dst", "edge_attr_3", "L0_gnn_W", "L0_gnn_a_src", "L0_gnn_a_dst", "L0_gnn_edge_W",
        "L0_gnn_edge_b", "L0_gnn_bias", "L0_ffn_router_w1", "L0_ffn_router_b1", "L0_ffn_router_w2",
        "L0_ffn_router_b2", "L0_ffn_expert_w1", "L0_ffn_expert_b1", "L0_ffn_expert_w2", "L0_ffn_expert_b2",
        "L0_ffn_expert_w3", "L0_ffn_expert_b3"]


def kernel(**inputs):
    import numpy as _np
    import concourse.bacc as _bacc
    from concourse import mybir as _mybir
    from concourse.bass_utils import run_bass_kernel_spmd as _run

    nc = _bacc.Bacc("TRN2", target_bir_lowering=False, num_devices=1)
    arrays, args = {}, []
    for name in _INS:
        a = _np.ascontiguousarray(inputs[name])
        arrays[f"in_{name}_dram"] = a
        args.append(nc.dram_tensor(f"in_{name}_dram", a.shape, _mybir.dt.from_np(a.dtype), kind="ExternalInput").ap())
    args.append(nc.dram_tensor("out_0_dram", (NODES, C), _mybir.dt.float32, kind="ExternalOutput").ap())
    bass_gnn_moe(nc, *args)
    r = _run(nc, [arrays], core_ids=[0])
    return r.results[0]["out_0_dram"]
```

```python
from contextlib import ExitStack

import numpy as np

import concourse.bass as bass
from concourse import mybir

ALU = mybir.AluOpType
ACT = mybir.ActivationFunctionType
AX = mybir.AxisListType
F32 = mybir.dt.float32
BF16 = mybir.dt.bfloat16
I32 = mybir.dt.int32
U32 = mybir.dt.uint32
ds = bass.ds

P = 128
NODES, C = 3125, 256
H, D = 8, 32
EDGES, EF = 50000, 3
NW = -(-NODES // P)
TAIL = NODES - (NW - 1) * P
EB = 256
NB = -(-EDGES // EB)
BC = NB // 2
NK = NB + NW - 1
NKP = 224
KC = NKP // 2
NSUB = 2 * NKP
CH = 16
G = NSUB // CH
SL = G * P
D1 = D + 1
CA = H * D1
HALL = H + CA
ROW = H + C
WSHIFT = 7
PAD_DST = 4095
BIG = 1e30
NE, RH = 6, 128
EPS = 1e-5
SPLIT_X = (0, 0, 0, 1, 1, 2)
SPLIT_W = (0, 1, 2, 0, 1, 0)
NPROD = len(SPLIT_X)
KE = NPROD * EF + NPROD
UN = 8
NI = NK // UN
REST = NK % UN
RU = 4
HR = 4
LAG = 2
GW = 4
NG = NW // GW
PA = (NG // 2 + 1) * GW
TW = 256
TB = TW // P
TWSHIFT = 8
TOPK = 2
NODE_COL = H - 1
NT = (TOPK * NODES + NE * (TW - 1)) // TW
RX = -(-NODES // P) * P + TW
SPARE = NE * RX
DUMP = SPARE + TW
TILE_DMAS = 6
UT = 4
NTP = -(-(NT + 2) // UT) * UT
assert NW % (2 * HR) == 1 and NW % GW == 1 and RU == GW and PA // GW == NG - PA // GW + 2
assert NB == 2 * BC and NKP % 2 == 0 and NSUB == CH * G and REST == RU and NKP >= NK + 4


def bass_gnn_moe(nc, x, src, dst, edge_attr, gnn_W, a_src, a_dst, edge_W, edge_b, gnn_bias,
                 router_w1, router_b1, router_w2, router_b2, expert_w1, expert_b1, expert_w2,
                 expert_b2, expert_w3, expert_b3, out):
    ctx = ExitStack()
    with ctx:
        def sb(name, shape, dt=F32):
            return ctx.enter_context(nc.sbuf_tensor(name, shape, dt))

        def sem(name):
            return ctx.enter_context(nc.semaphore(name))

        def sems(name, n):
            return [sem(f"{name}{i}") for i in range(n)]

        node_tab = nc.dram_tensor("node_tab", (NW * P, HALL), F32).ap()
        row_log = nc.dram_tensor("row_log", (NK, P, 2 * HALL), F32).ap()
        ea_log = nc.dram_tensor("ea_log", (NPROD * EF, NKP, EB), BF16).ap()
        expert_rows = nc.dram_tensor("expert_rows", (DUMP + TOPK * P, ROW), F32).ap()
        result = nc.dram_tensor("result", (NODES + TW, C), F32).ap()
        drel_log = nc.dram_tensor("drel_log", (NKP, EB), BF16).ap()

        banks = ctx.enter_context(nc.psum_tensor("banks", [P, 8, 512], F32))
        bank = [banks[:, i, :] for i in range(8)]

        ident = sb("ident", [P, P])
        iota_free = sb("iota_free", [P, NKP])
        iota_part = sb("iota_part", [P, 1])
        block_no = sb("block_no", [BC, 2])
        block_no128 = sb("block_no128", [BC, 2])
        step_no128 = sb("step_no128", [KC, 2])
        head_mask = sb("head_mask", [P, 2, H])
        bias_b = sb("bias_b", [P, C])
        rb2_b = sb("rb2_b", [P, NE])
        rw1 = sb("rw1", [P, 2, RH])
        rb1 = sb("rb1", [P, 1])
        rw2 = sb("rw2", [P, NE])
        eb12 = sb("eb12", [P, NE, 4])
        a_col = sb("a_col", [P, 2, 2])
        a_blk = sb("a_blk", [P, 2, 2, H])
        we = sb("we", [P, 2, EF + 1])
        we_bf = sb("we_bf", [P, 3, 2, EF + 1], BF16)
        we_res = sb("we_res", [P, 2, EF + 1])
        we_rows = sb("we_rows", [P, 2, KE])
        we_T = sb("we_T", [KE, C], BF16)
        w_all = sb("w_all", [P, 2, HALL])
        stats = sb("stats", [P, NW, 6])
        mean = sb("mean", [P, NW])
        rstd = sb("rstd", [P, NW])
        lt = sb("lt", [P, 3, NW])
        window_row = sb("window_row", [1, NKP], I32)
        window_f = sb("window_f", [P, NKP])
        drel_col = sb("drel_col", [P, NKP, 2])
        src_col = sb("src_col", [P, NKP, 2], I32)
        idx = sb("idx", [P, UN // 2, 4], I32)

        xs = sb("xs", [P, NW, C])
        big = sb("big", [P, NW * 3 * ROW // 2])
        h_parts = big[:, :].bitcast(BF16).rearrange("p (w s c) -> p w s c", w=NW, s=3)
        acc = big[:, 0:NW * ROW].rearrange("p (w c) -> p w c", w=NW)
        spare = [NW * ROW]

        def beside(shape, dt=F32):
            words = int(np.prod(shape[1:]))
            ap = big[0:shape[0], spare[0]:spare[0] + words]
            spare[0] += words
            assert spare[0] <= NW * 3 * CA // 2
            if dt != F32:
                ap = ap.bitcast(dt)
            return ap.rearrange("p (a b) -> p a b", a=shape[1]) if len(shape) == 3 else ap
        xn2 = beside([P, GW, C])
        lg = beside([P, NW, H])
        rsm = beside([P, 6, NW])
        top = beside([P, NW, 8])
        topi = beside([P, NW, 8], U32)
        topf = beside([P, NW, TOPK])
        pick1, pick2, places = (beside([P, NW, H]) for _ in range(3))
        NB_PART = max(PA, NW - PA)
        totals, sums_to, keep_w = (beside([P, H, NB_PART]) for _ in range(3))
        place_c = beside([P, NW])
        alpha = sb("alpha", [P, H, NSUB])
        slots = alpha[:, :, :].rearrange("p h s -> p s h")
        tiles_alpha = alpha[:, :, :].rearrange("p h s -> p (h s)")
        arena = sb("arena", [P, 4 * SL + 8])
        scan = [arena[:, i * SL + (8 if i > 1 else 0):(i + 1) * SL + (8 if i > 1 else 0)] for i in range(4)]
        resets = arena[:, SL:2 * SL + 1]

        def carve(start, shape, dt=F32):
            n = 1
            for s in shape[1:]:
                n *= s
            words = n if dt != BF16 else n // 2
            ap = arena[0:shape[0], start:start + words]
            if dt != F32:
                ap = ap.bitcast(dt)
            if len(shape) == 3:
                ap = ap.rearrange("p (a b) -> p a b", a=shape[1])
            if len(shape) == 4:
                ap = ap.rearrange("p (a b c) -> p a b c", a=shape[1], b=shape[2])
            return ap, start + words

        at = 0
        dst_i, at = carve(at, [BC, 2, EB], I32)
        src_i, at = carve(at, [BC, 2, EB], I32)
        prev_i, at = carve(at, [BC, 2], I32)
        ea_f, at = carve(at, [BC, 2, EB * EF])
        dst_f, at = carve(at, [BC, 2, EB])
        src_f, at = carve(at, [BC, 2, EB])
        last_w, at = carve(at, [BC, 2], I32)
        prev_w, at = carve(at, [BC, 2], I32)
        last_k, at = carve(at, [BC, 2])
        prev_k, at = carve(at, [BC, 2])
        sel_a, at = carve(at, [BC, 2, NKP])
        sel, at = carve(at, [BC, 2, NKP])
        drel_bf, at = carve(at, [KC, 2, EB], BF16)
        ea_r, at = carve(at, [KC, 2, EF, EB])
        ea_bf, at = carve(at, [KC, 2 * 3 * EF, EB], BF16)
        w_nat, at = carve(at, [P, 2, C])
        assert at <= 4 * SL
        at = 18 * 2 * C
        RING_TILE = (at - (2 * SL + 8)) // P
        gath, at = carve(at, [P, UN, 2, HALL])
        assert at <= 4 * SL
        ring_end = at
        w_tile, at = carve(0, [P, UT * 3, 2, C])
        b3_tile, at = carve(at, [P, UT, C])
        rows_in, at = carve(at, [P, UT * TB, ROW])
        xT2, at = carve(at, [P, 2, 2 * TW])
        hT1, at = carve(at, [P, 2, 2 * TW])
        hT2, at = carve(at, [P, 2, 2 * TW])
        y_out, at = carve(at, [P, 2 * TB, C])
        assert at <= ring_end
        pad_rows, at = carve(ring_end, [P, TB, ROW])
        assert at <= 4 * SL

        drel_b = sb("drel_b", [P, 2, 2, EB], BF16)
        ea_T = sb("ea_T", [KE, 2, 2, EB], BF16)
        hotT = sb("hotT", [P, RU, EB], BF16)
        head_copies = sb("head_copies", [CH, P])
        sums = sb("sums", [P, 2, 2, H])
        renc = sb("renc", [P, 2, 2, H, D1])
        prod = sb("prod", [P, 2, 2, H, D1 + 1])
        hot = prod[:, :, :, :, :].rearrange("p a b h d -> p (a b h d)")[:, 0:2 * RU * P].rearrange("p (a b n) -> p a b n", a=RU, b=2)
        xn = sb("xn", [P, 2, C])
        xT = sb("xT", [P, 2, 2, P])
        hf = sb("hf", [P, HR, HALL])
        hr = sb("hr", [P, ROW])
        msg = sb("msg", [P, RU, 2, ROW])
        rh = prod[:, :, :, :, :].rearrange("p a b h d -> p (a b h d)")[:, 0:GW * P]
        key_T = tiles_alpha
        key_16 = msg[:, :, :, :].rearrange("p a b c -> p (a b c)")[0:CH, 0:4 * 512].rearrange("p (a b) -> p a b", a=4)
        run = sb("run", [P, RU, ROW])
        keep = sb("keep", [P, NKP])
        xT_g = msg[:, :, :, :].rearrange("p a b c -> p (a b c)")[:, 0:2 * GW * P].rearrange("p (k n) -> p k n", k=2)
        row_ring = run
        ends = sb("ends", [P, 4])
        erow = sb("erow", [1, 4, P])
        dlink = sb("dlink", [1, 6, P])
        valid = sb("valid", [P, NSUB])
        key = sb("key", [P, NSUB])
        distance = key[:, 0:2 * P].rearrange("p (j n) -> p j n", j=2)
        carry = sb("carry", [1, 2, P])
        carry_c = sb("carry_c", [P, 2])
        rden = sb("rden", [P, GW, H])
        b12_tile = sb("b12_tile", [P, UT, 4])
        before = sb("before", [P, P])
        ones = sb("ones", [P, P])
        node_no = sb("node_no", [P, NW])
        is_node = sb("is_node", [P, NW])
        dump_row = sb("dump_row", [P, TOPK, NW])
        count_e = sb("count_e", [P, H])
        place = sb("place", [P, NW, TOPK], I32)
        place_idx = sb("place_idx", [P, RU, TOPK], I32)
        node_idx = sb("node_idx", [P, 2, TB], I32)
        tile_f = sb("tile_f", [1, 6, 8])
        tiles_i = sb("tiles_i", [1, 8], I32)
        pad_at = sb("pad_at", [1, 8], I32)
        tile_cmp = sb("tile_cmp", [1, 2, NTP * NE])
        tile_q = sb("tile_q", [1, 4, NTP])
        tile_expert = sb("tile_expert", [1, NTP], I32)
        tile_row = sb("tile_row", [1, NTP], I32)

        s_const = sem("s_const")
        s_pad = sem("s_pad")
        s_edges = sem("s_edges")
        s_x = sem("s_x")
        s_wt = sem("s_wt")
        s_wt2 = sem("s_wt2")
        s_dve = sem("s_dve")
        s_wps = sem("s_wps")
        s_wsb = sem("s_wsb")
        s_ablk = sem("s_ablk")
        s_we = sem("s_we")
        s_sel = sem("s_sel")
        s_selps = sem("s_selps")
        s_src = sem("s_src")
        s_logsrc = sem("s_logsrc")
        s_logs = sem("s_logs")
        s_var = sem("s_var")
        s_std = sem("s_std")
        s_bn = sem("s_bn")
        s_xn = sem("s_xn")
        s_xnT = sem("s_xnT")
        s_xT = sem("s_xT")
        s_hps = sem("s_hps")
        s_hf = sem("s_hf")
        s_split = sem("s_split")
        s_tab = sems("s_tab", HR)
        s_idx = sem("s_idx")
        s_g = sems("s_g", UN)
        s_log = sems("s_log", UN)
        s_drel = sems("s_drel", 2)
        s_ea = sems("s_ea", 2)
        s_hot = sem("s_hot")
        s_hd = sem("s_hd")
        s_enc = sem("s_enc")
        s_relu = sem("s_relu")
        s_prod = sem("s_prod")
        s_as = sem("s_as")
        s_sum = sem("s_sum")
        s_al = sem("s_al")
        s_key = sem("s_key")
        s_keyps = sem("s_keyps")
        s_keyc = sem("s_keyc")
        s_keyrep = sem("s_keyrep")
        s_keyT = sem("s_keyT")
        s_tp = sem("s_tp")
        s_tc = sem("s_tc")
        s_ends = sem("s_ends")
        s_row = sem("s_row")
        s_carry = sem("s_carry")
        s_dif = sem("s_dif")
        s_exp = sem("s_exp")
        s_bp = sem("s_bp")
        s_bc = sem("s_bc")
        s_ld = sems("s_ld", UN)
        s_oh = sem("s_oh")
        s_msg = sem("s_msg")
        s_exc = sem("s_exc")
        s_agg = sem("s_agg")
        s_acc = sem("s_acc")
        s_biased = sem("s_biased")
        s_put = sem("s_put")
        s_puta = sem("s_puta")
        s_oha = sem("s_oha")
        s_dist = sem("s_dist")
        s_prep = sem("s_prep")
        s_xn2 = sem("s_xn2")
        s_xkeep = sem("s_xkeep")
        s_t2 = sem("s_t2")
        s_xT2 = sem("s_xT2")
        s_rps = sem("s_rps")
        s_rh = sem("s_rh")
        s_lps = sem("s_lps")
        s_soft = sem("s_soft")
        s_softe = sem("s_softe")
        s_gap = sem("s_gap")
        s_gape = sem("s_gape")
        s_pick = sem("s_pick")
        s_rank = sem("s_rank")
        s_place = sem("s_place")
        s_stage = sem("s_stage")
        s_pidx = sem("s_pidx")
        s_scat = sems("s_scat", RU)
        s_scattered = sem("s_scattered")
        s_table = sem("s_table")
        s_pads = sem("s_pads")
        s_tile = sems("s_tile", UT)
        s_Tt = sem("s_Tt")
        s_xTt = sem("s_xTt")
        s_l1 = sem("s_l1")
        s_h1 = sem("s_h1")
        s_l2 = sem("s_l2")
        s_h2 = sem("s_h2")
        s_l3 = sem("s_l3")
        s_yb = sem("s_yb")
        s_y = sem("s_y")
        s_add = sems("s_add", 2)
        s_added = sem("s_added")
        s_out = sem("s_out")
        s_gate_act, s_gate_pe, s_gate_pool, s_gate_dve = (sem(f"s_gate_{n}") for n in ("act", "pe", "pool", "dve"))

        def flat(ap):
            return ap.rearrange("p a c -> p (a c)")

        def tiles_of(n):
            return -(-n // P)

        def first(i):
            return isinstance(i, int) and i == 0

        def windows(eng, body):
            def round_of_two(i, q, lap):
                body(i, 0, q, lap)
                body(i, 1, q + 1, lap)
            round_of_two(0, 0, 0)
            round_of_two(1, 2, 0)
            round_of_two(2, 0, 1)
            with eng.Fori(1, (NW // 2 - 2) // 2) as n:
                round_of_two(2 * n + 1, 2, n)
                round_of_two(2 * n + 2, 0, n + 1)
            round_of_two(NW // 2 - 1, 2, NW // HR - 1)
            body(NW // 2, 0, 0, NW // HR)

        def inside(w):
            return not isinstance(w, int) or w < NW

        block = ctx.enter_context(nc.Block())

        @block.sync
        def _(sp):
            sp.wait_ge(s_pad, 5)
            full = (NB - 1) * EB
            for t, v in ((dst_i, dst), (src_i, src)):
                sp.dma_start(t[:, 0, :], v[0:BC * EB].rearrange("(p e) -> p e", p=BC)).then_inc(s_edges, 16)
                sp.dma_start(t[0:BC - 1, 1, :], v[BC * EB:full].rearrange("(p e) -> p e", p=BC - 1)).then_inc(s_edges, 16)
                sp.dma_start(t[BC - 1:BC, 1, 0:EDGES - full], v[full:EDGES].rearrange("(a e) -> a e", a=1)).then_inc(s_edges, 16)
            whole = dst[0:full].rearrange("(t e) -> t e", e=EB)
            with nc.allow_non_contiguous_dma("one word per block"):
                sp.dma_start(prev_i[1:BC, 0:1], whole[0:BC - 1, EB - 1:EB]).then_inc(s_edges, 16)
                sp.dma_start(prev_i[0:BC, 1:2], whole[BC - 1:NB - 1, EB - 1:EB]).then_inc(s_edges, 16)
            ev = edge_attr.rearrange("e c -> (e c)")
            EL = EB * EF
            sp.dma_start(ea_f[:, 0, :], ev[0:BC * EL].rearrange("(p e) -> p e", p=BC)).then_inc(s_edges, 16)
            sp.dma_start(ea_f[0:BC - 1, 1, :], ev[BC * EL:(NB - 1) * EL].rearrange("(p e) -> p e", p=BC - 1)).then_inc(s_edges, 16)
            sp.dma_start(ea_f[BC - 1:BC, 1, 0:EDGES * EF - (NB - 1) * EL],
                         ev[(NB - 1) * EL:EDGES * EF].rearrange("(a e) -> a e", a=1)).then_inc(s_edges, 16)
            sp.dma_start(xs[:, 0:NW - 1, :], x[0:(NW - 1) * P, :].rearrange("(w p) c -> p w c", p=P)).then_inc(s_x, 16)
            sp.dma_start(xs[0:TAIL, NW - 1, :], x[(NW - 1) * P:NODES, :]).then_inc(s_x, 16)

            sp.wait_ge(s_logsrc, 1)
            for kb in range(2):
                sp.dma_start(drel_log[kb * KC:(kb + 1) * KC, :], drel_bf[:, kb, :]).then_inc(s_logs, 16)
                for q in range(NPROD):
                    a = kb * 9 + SPLIT_X[q] * EF
                    sp.dma_start(ea_log[q * EF:(q + 1) * EF, kb * KC:(kb + 1) * KC, :].rearrange("c k e -> k c e"),
                                 ea_bf[:, a:a + EF, :]).then_inc(s_logs, 16)

            def table(i, slot, q, lap):
                w = 2 * i + slot
                sp.wait_ge(s_hf, w + 3)
                sp.dma_start(node_tab[ds(w * P, P), :], hf[:, q, :]).then_inc(s_tab[q], 16)
            windows(sp, table)

            sp.wait_ge(s_logs, 16 * 2 * (1 + NPROD))

            def load_pair(q, p):
                if not (isinstance(q, int) and q < 2):
                    sp.wait_ge(s_hot, 2 * q)
                    sp.wait_ge(s_enc, 2 * q)
                sp.dma_start(drel_b[:, p, :, :], drel_log[ds(2 * q, 2), :].partition_broadcast(P)).then_inc(s_drel[p], 16)
                sp.dma_start(ea_T[0:NPROD * EF, p, :, :], ea_log[:, ds(2 * q, 2), :]).then_inc(s_ea[p], 16)

            def log_rows(i, n):
                for u in range(n):
                    if u % 2 == 0:
                        load_pair(UN // 2 * i + (u // 2 + 2), u // 2 % 2)
                    sp.wait_ge(s_g[u], 32 * i + 32)
                    sp.dma_start(flat(row_log[ds(UN * i + u, 1), :, :].rearrange("k p c -> p k c")),
                                 flat(gath[:, u, :, :])).then_inc(s_log[u], 16)
            load_pair(0, 0)
            load_pair(1, 1)
            with sp.Fori(0, NI) as i:
                log_rows(i, UN)
            log_rows(NI, REST)
            for p in range(2):
                sp.wait_ge(s_drel[p], 16 * (NK // 4 + 1))
                sp.wait_ge(s_ea[p], 16 * (NK // 4 + 1))
            for u in range(UN):
                sp.wait_ge(s_log[u], 16 * (NI + (u < REST)))

            sp.wait_ge(s_bp, G // 4)

            def load_rows(i, n):
                for u in range(n):
                    sp.wait_ge(s_msg, UN * i + u + 1)
                    sp.dma_start(flat(gath[:, u, :, :]),
                                 flat(row_log[ds(UN * i + u, 1), :, :].rearrange("k p c -> p k c"))).then_inc(s_ld[u], 16)
            with sp.Fori(0, NI) as i:
                load_rows(i, UN)
            load_rows(NI, REST)
            sp.wait_ge(s_xn2, NG + 1)
            sp.dma_start(result[0:(NW - 1) * P, :].rearrange("(w p) c -> p w c", p=P), xs[:, 0:NW - 1, :]).then_inc(s_pads, 16)
            sp.dma_start(result[(NW - 1) * P:NODES, :], xs[0:TAIL, NW - 1, :]).then_inc(s_pads, 16)
            sp.dma_start(result[NODES:NODES + TW, :].rearrange("(j p) c -> p j c", p=P), pad_rows[:, :, H:ROW]).then_inc(s_pads, 16)
            sp.dma_start(expert_rows[SPARE:SPARE + TW, :].rearrange("(j p) c -> p j c", p=P), pad_rows).then_inc(s_pads, 16)
            sp.wait_ge(s_table, 1)
            for e in range(NE):
                at_row = sp.value_load(pad_at[0:1, e:e + 1], min_val=0, max_val=SPARE - TW)
                sp.dma_start(expert_rows[ds(at_row, TW), :].rearrange("(j p) c -> p j c", p=P), pad_rows).then_inc(s_pads, 16)

            def load_expert(t, u):
                e = sp.value_load(tile_expert[0:1, ds(t, 1)], min_val=0, max_val=NE - 1)
                sp.wait_ge(s_y, t + 1)
                for n, w in enumerate((expert_w1, expert_w2, expert_w3)):
                    sp.dma_start(w_tile[:, u * 3 + n, :, :], w[ds(e, 1), :, :].rearrange("x (a p) f -> p (x a) f", p=P)).then_inc(s_tile[u], 16)
                sp.dma_start(b12_tile[:, u, :], flat(eb12[:, ds(e, 1), :])).then_inc(s_tile[u], 16)
                sp.dma_start(b3_tile[:, u, :], flat(expert_b3[ds(e, 1), :].partition_broadcast(P))).then_inc(s_tile[u], 16)

            def load_rows_of(t, u):
                row = sp.value_load(tile_row[0:1, ds(t, 1)], min_val=0, max_val=SPARE)
                sp.dma_start(rows_in[:, u * TB:(u + 1) * TB, :], expert_rows[ds(row, TW), :].rearrange("(j p) c -> p j c", p=P)).then_inc(s_tile[u], 16)
            for u in range(UT):
                load_expert(u, u)
            sp.wait_ge(s_pads, 16 * (4 + NE))
            sp.wait_ge(s_scattered, 1)
            for u in range(UT):
                load_rows_of(u, u)
            with sp.Fori(1, NTP // UT) as i:
                for u in range(UT):
                    load_expert(UT * i + u, u)
                    load_rows_of(UT * i + u, u)
            for u in range(UT):
                sp.wait_ge(s_tile[u], 16 * TILE_DMAS * (NTP // UT))
            sp.wait_ge(s_added, 2 + NT)
            sp.dma_start(out, result[0:NODES, :]).then_inc(s_out, 16)
            sp.wait_ge(s_out, 16)

        @block.gpsimd
        def _(pool):
            pool.memset(dst_i, PAD_DST).then_inc(s_pad, 1)
            pool.memset(src_i, 0).then_inc(s_pad, 1)
            pool.memset(prev_i, 0).then_inc(s_pad, 1)
            pool.memset(ea_f, 0.0).then_inc(s_pad, 1)
            pool.memset(xs[:, NW - 1, :], 0.0).then_inc(s_pad, 1)
            pool.memset(ident[:, :], 0.0).then_inc(s_const, 1)
            for t, pattern, mul in ((iota_free, [[1, NKP]], 0), (iota_part, [[0, 1]], 1), (block_no, [[BC, 2]], 1),
                                    (block_no128, [[BC * P, 2]], P), (step_no128, [[KC * P, 2]], P)):
                pool.iota(t[:, :], pattern, 0, mul, allow_small_or_imprecise_dtypes=True).then_inc(s_const, 1)
            pool.memset(head_mask[:, :, :], 0.0).then_inc(s_const, 1)
            pool.memset(ea_T[:, :, :, :], 1.0).then_inc(s_const, 1)
            pool.wait_ge(s_const, 8)
            pool.affine_select(out=ident[:, :], in_=ident[:, :], compare_op=ALU.not_equal, fill=1.0,
                               base=0, pattern=[[-1, P]], channel_multiplier=1).then_inc(s_const, 1)

            for q in range(HR):
                pool.wait_ge(s_tab[q], 16 * (NW // HR + (q < NW % HR)))
            pool.wait_ge(s_src, 1)

            def stage_indices(k, p):
                pool.wait_ge(s_al, k + 2)
                pool.sem_inc(s_gate_pool, 1)
                pool.tensor_copy(idx[:, p, :], src_col[:, ds(k, 2), :].rearrange("p a b -> p (a b)")).then_inc(s_idx, 1)

            def gather(i, n):
                for p in range(n // 2):
                    stage_indices(UN * i + (2 * p + 2), (p + 1) % (UN // 2))
                    pool.wait_ge(s_al, UN * i + 2 * p + 2)
                    pool.wait_ge(s_idx, UN // 2 * i + p + 1)
                    for u in (2 * p, 2 * p + 1):
                        if not first(i):
                            pool.wait_ge(s_log[u], 16 * i)
                        pool.sem_inc(s_gate_pool, 1)
                        for j in range(2):
                            c = 2 * (u % 2) + j
                            pool.indirect_dma_start(
                                out=gath[:, u, j, :], out_offset=None, in_=node_tab[:, :],
                                in_offset=bass.IndirectOffsetOnAxis(ap=idx[:, p, c:c + 1], axis=0)).then_inc(s_g[u], 16)
            pool.wait_ge(s_logs, 16 * 2 * (1 + NPROD))
            stage_indices(0, 0)
            gather(0, UN)
            with pool.Fori(1, NI) as i:
                gather(i, UN)
            gather(NI, REST)

            pool.wait_ge(s_wt2, 16 * (1 + 2 * NE + 4))
            for w in range(0, NW, GW):
                n = min(GW, NW - w)
                b = pool.tensor_tensor(xs[:, w:w + n, :], xs[:, w:w + n, :], bias_b[:, :].unsqueeze(1).broadcast_to([P, n, C]), ALU.add)
            b.then_inc(s_biased, 1)

            pool.sem_inc(s_put, 2)
            pool.wait_ge(s_hd, 3 + NK)

            def put(k, v, half):
                w = pool.value_load(window_row[0:1, ds(k, 1)], min_val=0, max_val=NW - 1)
                pool.wait_ge(s_acc, k + RU + 1)
                pool.wait_ge(s_puta, half + 2)
                pool.sem_inc(s_gate_pool, 1)
                pool.tensor_copy(flat(acc[:, ds(w, 1), :]), run[:, v, :]).then_inc(s_put, 1)
            with pool.Fori(0, NK // RU) as i:
                for v in range(0, RU, 2):
                    put(RU * i + v, v, RU // 2 * i + v // 2)

            def scatter(i, v):
                w = RU * i + v
                pool.wait_ge(s_stage, w + RU + 1)
                if not first(i):
                    pool.wait_ge(s_scat[v], 16 * TOPK * i)
                pool.sem_inc(s_gate_pool, 1)
                pool.tensor_copy(place_idx[:, v, :], flat(place[:, ds(w, 1), :])).then_inc(s_pidx, 1)
                pool.wait_ge(s_pidx, w + 1)
                pool.sem_inc(s_gate_pool, 1)
                for c in range(TOPK):
                    pool.indirect_dma_start(
                        out=expert_rows[:, :], out_offset=bass.IndirectOffsetOnAxis(ap=place_idx[:, v, c:c + 1], axis=0),
                        in_=row_ring[:, v, :], in_offset=None).then_inc(s_scat[v], 16)
            for v in range(RU):
                scatter(0, v)
            with pool.Fori(1, NW // RU) as i:
                for v in range(RU):
                    scatter(i, v)
            scatter(NW // RU, 0)
            for v in range(RU):
                pool.wait_ge(s_scat[v], 16 * TOPK * (NW // RU + (v < NW % RU)))
            pool.sem_inc(s_scattered, 1)

            pool.sem_inc(s_added, 2)

            def add_tile(t, v):
                pool.wait_ge(s_y, t + UT + 1)
                pool.sem_inc(s_gate_pool, 1)
                for j in range(TB):
                    pool.indirect_dma_start(
                        out=result[:, :], out_offset=bass.IndirectOffsetOnAxis(ap=node_idx[:, v, j:j + 1], axis=0),
                        in_=y_out[:, v * TB + j, :], in_offset=None, compute_op=ALU.add).then_inc(s_add[v], 16)

            with pool.Fori(0, NT // 2) as i:
                for v in range(2):
                    add_tile(2 * i + v, v)
                    pool.wait_ge(s_add[v], 16 * TB * i + 16 * TB)
                    pool.sem_inc(s_added, 1)

        @block.scalar
        def _(act):
            for s, depth in ((s_xT, 2), (s_hf, 2), (s_relu, 2),  (s_xkeep, 1), (s_stage, RU), (s_xTt, 2), (s_h1, 2), (s_h2, 2)):
                act.sem_inc(s, depth)
            act.dma_start(w_nat, gnn_W.rearrange("(a p) k -> p a k", p=P)).then_inc(s_wt, 16)
            with nc.allow_non_contiguous_dma("small weight columns"):
                act.dma_start(a_col[:, :, 0], a_src.rearrange("h d -> (h d)").rearrange("(a p) -> p a", p=P)).then_inc(s_wt, 16)
                act.dma_start(a_col[:, :, 1], a_dst.rearrange("h d -> (h d)").rearrange("(a p) -> p a", p=P)).then_inc(s_wt, 16)
                act.dma_start(we[:, :, 0:EF], edge_W.rearrange("(a p) c -> p a c", p=P)).then_inc(s_wt, 16)
                act.dma_start(we[:, :, EF], edge_b.rearrange("(a p) -> p a", p=P)).then_inc(s_wt, 16)
                act.dma_start(rb1[:, :], router_b1.rearrange("(p a) -> p a", a=1)).then_inc(s_wt2, 16)
                for e in range(NE):
                    act.dma_start(eb12[:, e, 0:2], expert_b1[e, :].rearrange("(a p) -> p a", p=P)).then_inc(s_wt2, 16)
                    act.dma_start(eb12[:, e, 2:4], expert_b2[e, :].rearrange("(a p) -> p a", p=P)).then_inc(s_wt2, 16)
            act.dma_start(bias_b[:, :], gnn_bias.partition_broadcast(P)).then_inc(s_wt2, 16)
            act.dma_start(rb2_b[:, :], router_b2.partition_broadcast(P)).then_inc(s_wt2, 16)
            act.dma_start(rw1[:, :, :], router_w1.rearrange("(a p) f -> p a f", p=P)).then_inc(s_wt2, 16)
            act.dma_start(rw2[:, :], router_w2).then_inc(s_wt2, 16)

            act.wait_ge(s_wps, 1)
            for kb in range(2):
                heads = w_all[:, kb, H:HALL].rearrange("p (h d) -> p h d", h=H)
                a = act.activation(heads[:, :, 0:D], bank[7][:, kb * C:(kb + 1) * C].rearrange("p (h d) -> p h d", h=H), ACT.Copy)
            a.then_inc(s_wsb, 1)
            act.wait_ge(s_wps, 2)
            pa = bank[6][:, 0:32].rearrange("p (k s h) -> p k s h", k=2, s=2)
            act.activation(w_all[:, :, 0:H], pa[:, :, 0, :], ACT.Copy).then_inc(s_wsb, 1)
            act.activation(w_all[:, :, H + D:HALL:D1], pa[:, :, 1, :], ACT.Copy).then_inc(s_wsb, 1)
            act.wait_ge(s_wps, 3)
            act.activation(we_T[:, :], bank[5][0:KE, 0:C], ACT.Copy).then_inc(s_wsb, 1)

            def copy_keys(n):
                act.wait_ge(s_keyps, n + 1)
                if n >= 4:
                    act.wait_ge(s_keyrep, n - 3)
                act.activation(key_16[:, n % 4, :], bank[n % 2][0:CH, :], ACT.Copy).then_inc(s_keyc, 1)
            copy_keys(0)
            for n in range(G // 4):
                if n + 1 < G // 4:
                    copy_keys(n + 1)
                act.wait_ge(s_keyrep, n + 1)
                act.activation(key_T[:, n * 4 * P:(n + 1) * 4 * P], bank[2 + n % 2], ACT.Copy).then_inc(s_keyT, 1)

            act.wait_ge(s_var, 1)
            act.activation(rstd[:, :], lt[:, 0, :], ACT.Sqrt).then_inc(s_std, 1)

            def copy_turned(w, slot):
                act.wait_ge(s_xnT, w + 3)
                act.wait_ge(s_hps, w + 1)
                act.sem_inc(s_gate_act, 1)
                act.activation(xT[:, slot, :, :], bank[slot][:, 0:C].rearrange("p (k n) -> p k n", k=2), ACT.Copy).then_inc(s_xT, 1)

            def project(i, slot, q, lap):
                w = 2 * i + slot
                if inside(w + 1):
                    copy_turned(w + 1, 1 - slot)
                act.wait_ge(s_hps, w + 3)
                if not first(lap):
                    act.wait_ge(s_tab[q], 16 * lap)
                act.wait_ge(s_split, 4 * w + 2)
                act.sem_inc(s_gate_act, 1)
                act.activation(hf[:, q, :], bank[2 + slot][:, 0:HALL], ACT.Copy).then_inc(s_hf, 1)
            copy_turned(0, 0)
            windows(act, project)

            def relu(k, v):
                act.wait_ge(s_enc, k + 3)
                act.wait_ge(s_prod, k + 1)
                act.sem_inc(s_gate_act, 1)
                act.activation(renc[:, v, :, :, 0:D], bank[4 + v].rearrange("p (j h d) -> p j h d", j=2, h=H), ACT.Relu).then_inc(s_relu, 1)

            def source_logits(k, u, kg):
                act.wait_ge(s_g[u], 32 * kg)
                act.wait_ge(s_al, k + UN - 1)
                act.sem_inc(s_gate_act, 1)
                act.activation(prod[:, u % 2, :, :, D1], gath[:, u, :, 0:H], ACT.Copy).then_inc(s_as, 1)
            def first_phase(i, n):
                for u in range(n):
                    relu(UN * i + u + 1, (u + 1) % 2)
                    source_logits(UN * i + u, u, i + 1)
            relu(0, 0)
            with act.Fori(0, NI) as i:
                first_phase(i, UN)
            first_phase(NI, REST)

            for n in range(G // 4):
                if n == RING_TILE // 4:
                    for u in range(UN):
                        act.wait_ge(s_log[u], 16 * (NI + (u < REST)))
                act.wait_ge(s_tp, n + 1)
                act.activation(scan[2][:, n * 4 * P:(n + 1) * 4 * P], bank[n], ACT.Copy).then_inc(s_tc, 1)
            HALF = G // 4 // 2 * 4
            for part, (a, b) in enumerate(((0, HALF), (HALF, G))):
                act.wait_ge(s_dif, part + 1)
                act.activation(scan[0][:, a * P:b * P], scan[2][:, a * P:b * P], ACT.Exp).then_inc(s_exp, 1)
            for n in range(G // 4):
                act.wait_ge(s_bp, n + 1)
                for g in range(4 * n, 4 * n + 4):
                    a = act.activation(tiles_alpha[:, g::G], bank[n][:, g % 4 * P:(g % 4 + 1) * P], ACT.Copy)
                a.then_inc(s_bc, 1)
            act.wait_ge(s_bc, G // 4)
            def beside_messages(k, v, half):
                act.wait_ge(s_agg, k + 1)
                if v % 2:
                    act.wait_ge(s_oha, half)
                act.sem_inc(s_gate_act, 1)
                act.activation(msg[:, v, :, 0:H], slots[:, ds(2 * k, 2), :], ACT.Copy).then_inc(s_exc, 1)
                if v % 2:
                    for j in range(2):
                        a = act.activation(distance[:, j, :], iota_free[:, 0:P], ACT.Abs, bias=flat(drel_col[:, ds(k, 1), j:j + 1]), scale=-1.0)
                    a.then_inc(s_dist, 1)
                    act.wait_ge(s_dist, half + 1)
                    act.activation(hot[:, v, :, :], distance, ACT.Relu, bias=1.0, scale=-1.0).then_inc(s_oha, 1)

            def put(k, v, half):
                w = act.value_load(window_row[0:1, ds(k, 1)], min_val=0, max_val=NW - 1)
                act.wait_ge(s_acc, k + RU + 1)
                act.wait_ge(s_put, half + 3)
                act.sem_inc(s_gate_act, 1)
                act.activation(flat(acc[:, ds(w, 1), :]), run[:, v, :], ACT.Copy).then_inc(s_puta, 1)

            act.sem_inc(s_puta, 2)
            for v in range(RU):
                beside_messages(v, v, v // 2)
            with act.Fori(1, NK // RU) as i:
                for v in range(RU):
                    beside_messages(RU * i + v, v, RU // 2 * i + v // 2)
                    if v % 2:
                        put(RU * i + (v - RU), v, RU // 2 * i + (v - RU) // 2)
            for k in range(NK - RU + 1, NK, 2):
                put(k, k % RU, k // 2)

            act.wait_ge(s_wt2, 16 * (1 + 2 * NE + 4))

            def deviation(g):
                act.wait_ge(s_var, g + 2)
                act.activation(rstd[:, 0:GW], lt[:, 0, 0:GW], ACT.Sqrt).then_inc(s_std, 1)

            def features(g, tiles):
                act.wait_ge(s_xn2, g + 1)
                act.sem_inc(s_gate_act, 1)
                act.activation(acc[:, ds(g * GW, tiles), H:ROW], xn2[:, 0:tiles, :], ACT.Copy).then_inc(s_xkeep, 1)
                act.wait_ge(s_t2, g + 2)
                act.sem_inc(s_gate_act, 1)
                act.activation(xT_g[:, :, 0:tiles * P], banks[:, 0:2, 0:tiles * P], ACT.Copy).then_inc(s_xT2, 1)

            def hidden(g, tiles):
                act.wait_ge(s_rps, g + 1)
                act.sem_inc(s_gate_act, 1)
                act.activation(rh[:, 0:tiles * P], bank[2][:, 0:tiles * P], ACT.Relu, bias=rb1[:, 0:1]).then_inc(s_rh, 1)

            def choose(part, w0, n):
                act.wait_ge(s_soft, part + 1)
                act.activation(lg[:, w0:w0 + n, 0:NE], lg[:, w0:w0 + n, 0:NE], ACT.Exp).then_inc(s_softe, 1)
                act.wait_ge(s_gap, part + 1)
                act.activation(rsm[:, 2, w0:w0 + n], rsm[:, 1, w0:w0 + n], ACT.Exp).then_inc(s_gape, 1)

            def stage(i, v):
                w = RU * i + v
                if not first(i):
                    act.wait_ge(s_scat[v], 16 * TOPK * i)
                act.sem_inc(s_gate_act, 1)
                act.activation(row_ring[:, v, :], flat(acc[:, ds(w, 1), :]), ACT.Copy).then_inc(s_stage, 1)

            def group(g):
                features(g, GW)
                deviation(g + 1)
                hidden(g, GW)

            deviation(0)
            with act.Fori(0, PA // GW - 1) as g:
                group(g)
            features(PA // GW - 1, GW)
            hidden(PA // GW - 1, GW)
            choose(0, 0, PA)
            deviation(PA // GW)
            act.wait_ge(s_place, 1)
            for v in range(RU):
                stage(0, v)
            for i in range(1, PA // RU - 2):
                group(i + (PA // GW - 1))
                for v in range(RU):
                    stage(i, v)
            group(NG - 1)
            features(NG, 1)
            hidden(NG, 1)
            for v in range(RU):
                stage(PA // RU - 2, v)
            choose(1, PA, NW - PA)
            for v in range(RU):
                stage(PA // RU - 1, v)
            act.wait_ge(s_place, 2)
            with act.Fori(PA // RU, NW // RU) as i:
                for v in range(RU):
                    stage(i, v)
            stage(NW // RU, 0)

            def turned(t, u, v):
                act.wait_ge(s_Tt, t + 1)
                act.wait_ge(s_l1, t + 1)
                act.sem_inc(s_gate_act, 1)
                act.activation(xT2[:, v, :], bank[6 + v], ACT.Copy).then_inc(s_xTt, 1)

            def layer1(t, u, v):
                act.wait_ge(s_l1, t + 3)
                act.wait_ge(s_l2, t + 1)
                act.sem_inc(s_gate_act, 1)
                for m in range(2):
                    a = act.activation(hT1[:, v, m * TW:(m + 1) * TW], bank[v][:, m * TW:(m + 1) * TW], ACT.Relu, bias=b12_tile[:, u, m:m + 1])
                a.then_inc(s_h1, 1)

            def layer2(t, u, v):
                act.wait_ge(s_l2, t + 3)
                act.wait_ge(s_l3, t + 1)
                act.sem_inc(s_gate_act, 1)
                for m in range(2):
                    a = act.activation(hT2[:, v, m * TW:(m + 1) * TW], bank[2 + v][:, m * TW:(m + 1) * TW], ACT.Relu, bias=b12_tile[:, u, 2 + m:3 + m])
                a.then_inc(s_h2, 1)

            def tiles(i, n):
                for u in range(n):
                    t = UT * i + u
                    layer2(t, u, u % 2)
                    turned(t + 2, (u + 2) % UT, u % 2)
                    layer1(t + 1, (u + 1) % UT, (u + 1) % 2)
            turned(0, 0, 0)
            turned(1, 1, 1)
            layer1(0, 0, 0)
            with act.Fori(0, NT // UT) as i:
                tiles(i, UT)
            tiles(NT // UT, NT % UT)

        @block.tensor
        def _(pe):
            mm = pe.matmul
            for s, depth in ((s_xnT, 2), (s_hps, 2), (s_enc, 2), (s_hd, 3), (s_agg, RU), (s_t2, 1), (s_l1, 2), (s_l2, 2), (s_l3, 2)):
                pe.sem_inc(s, depth)
            pe.wait_ge(s_const, 9)
            pe.wait_ge(s_wt, 80)
            for kb in range(2):
                for ob in range(2):
                    t = pe.transpose(bank[7][:, kb * C + ob * P:kb * C + (ob + 1) * P], w_nat[:, ob, kb * P:(kb + 1) * P], ident[:, :])
            t.then_inc(s_wps, 1)
            pe.wait_ge(s_ablk, 1)
            for kb in range(2):
                for ob in range(2):
                    t = mm(bank[6][:, kb * 16:kb * 16 + 16], w_nat[:, ob, kb * P:(kb + 1) * P],
                           a_blk[:, ob, :, :].rearrange("p a h -> p (a h)"), start=ob == 0, stop=ob == 1)
            t.then_inc(s_wps, 1)
            pe.wait_ge(s_we, 1)
            for ob in range(2):
                t = pe.transpose(bank[5][0:KE, ob * P:(ob + 1) * P], we_rows[:, ob, :], ident[:, :])
            t.then_inc(s_wps, 1)

            pe.wait_ge(s_sel, 1)
            pe.wait_ge(s_wsb, 4)
            for a in range(2):
                t = mm(bank[0][:, 0:NKP], block_no[:, a:a + 1].broadcast_to([BC, P]), sel[:, a, :], start=a == 0, stop=a == 1)
            t.then_inc(s_selps, 1)
            for j in range(2):
                for a in range(2):
                    t = mm(bank[3][:, j * NKP:(j + 1) * NKP], src_f[:, a, j * P:(j + 1) * P], sel[:, a, :], start=a == 0, stop=a == 1)
            t.then_inc(s_selps, 1)
            for j in range(2):
                for a in range(2):
                    t = mm(bank[2][:, j * NKP:(j + 1) * NKP], dst_f[:, a, j * P:(j + 1) * P], sel[:, a, :], start=a == 0, stop=a == 1)
            t.then_inc(s_selps, 1)
            for kb in range(2):
                for a in range(2):
                    t = mm(bank[1][0:KC, kb * EB:(kb + 1) * EB], sel[:, a, kb * KC:(kb + 1) * KC], dst_f[:, a, :], start=a == 0, stop=a == 1)
            t.then_inc(s_selps, 1)
            for c in range(EF):
                for kb in range(2):
                    for a in range(2):
                        t = mm(bank[4 + c][0:KC, kb * EB:(kb + 1) * EB], sel[:, a, kb * KC:(kb + 1) * KC],
                               ea_f[:, a, :].rearrange("p (e c) -> p c e", c=EF)[:, c, :], start=a == 0, stop=a == 1)
                t.then_inc(s_selps, 1)

            def turn_keys(n):
                if n >= 2:
                    pe.wait_ge(s_keyc, n - 1)
                for q in range(4):
                    t = pe.transpose(bank[n % 2][0:CH, q * P:(q + 1) * P], key[:, 4 * n + q::G], ident[:, :])
                t.then_inc(s_keyps, 1)
            pe.wait_ge(s_key, 1)
            turn_keys(0)
            for n in range(G // 4):
                if n + 1 < G // 4:
                    turn_keys(n + 1)
                pe.wait_ge(s_keyc, n + 1)
                if n >= 2:
                    pe.wait_ge(s_keyT, n - 1)
                mm(bank[2 + n % 2], head_copies[:, :], key_16[:, n % 4, :], start=True, stop=True).then_inc(s_keyrep, 1)
            pe.wait_ge(s_keyT, G // 4)

            def turn_window(w, slot):
                pe.wait_ge(s_xn, w + 1)
                pe.wait_ge(s_xT, w + 1)
                pe.sem_inc(s_gate_pe, 1)
                for kb in range(2):
                    t = pe.transpose(bank[slot][:, kb * P:(kb + 1) * P], xn[:, slot, kb * P:(kb + 1) * P], ident[:, :])
                t.then_inc(s_xnT, 1)

            def project(i, slot, q, lap):
                w = 2 * i + slot
                if inside(w + 1):
                    turn_window(w + 1, 1 - slot)
                pe.wait_ge(s_xT, w + 3)
                pe.wait_ge(s_hf, w + 1)
                pe.sem_inc(s_gate_pe, 1)
                for kb in range(2):
                    t = mm(bank[2 + slot][:, 0:HALL], xT[:, slot, kb, :], w_all[:, kb, :], start=kb == 0, stop=kb == 1)
                t.then_inc(s_hps, 1)
            turn_window(0, 0)
            windows(pe, project)

            pe.wait_ge(s_xT, 2 + NW)
            pe.wait_ge(s_logsrc, 1)
            pe.wait_ge(s_hf, 2 + NW)
            pe.wait_ge(s_split, 8 + 4 * NW)

            def encode(k, u, kp):
                v = u % 2
                pe.wait_ge(s_ea[u // 2], 16 * kp + 16)
                pe.wait_ge(s_relu, k + 1)
                pe.sem_inc(s_gate_pe, 1)
                for j in range(2):
                    t = mm(bank[4 + v][:, j * C:(j + 1) * C], ea_T[:, u // 2, v, j * P:(j + 1) * P], we_T[:, :], start=True, stop=True)
                t.then_inc(s_enc, 1)

            def look_up(k, u, w):
                v = u % 2
                pe.wait_ge(s_hot, k + 3)
                pe.wait_ge(s_prod, k + 1)
                pe.sem_inc(s_gate_pe, 1)
                for j in range(2):
                    for s in range(3):
                        t = mm(bank[2 * v + j][:, 0:CA], hotT[:, u, j * P:(j + 1) * P], flat(h_parts[:, ds(w, 1), s, :]),
                               start=s == 0, stop=s == 2)
                t.then_inc(s_hd, 1)

            encode(0, 0, 0)
            with pe.Fori(0, NK // 4) as i:
                for u in range(4):
                    w = pe.value_load(window_row[0:1, ds(4 * i + u, 1)], min_val=0, max_val=NW - 1)
                    encode(4 * i + (u + 1), (u + 1) % 4, i + (u + 1) // 4)
                    look_up(4 * i + u, u, w)

            pe.wait_ge(s_al, UN + NK)
            pe.wait_ge(s_relu, 2 + NK + 1)
            for g in range(G):
                t = pe.transpose(bank[g // 4][:, g % 4 * P:(g % 4 + 1) * P], tiles_alpha[:, g::G], ident[:, :])
                if g % 4 == 3:
                    t.then_inc(s_tp, 1)
            pe.wait_ge(s_tc, G // 4)
            pe.wait_ge(s_ends, 1)
            for c in range(4):
                t = pe.transpose(bank[0][0:1, c * P:(c + 1) * P], ends[:, c:c + 1], ident[:, :])
            t.then_inc(s_row, 1)
            pe.wait_ge(s_carry, 1)
            for c in range(2):
                t = pe.transpose(bank[1][:, c:c + 1], carry[0:1, c, :], ident[0:1, 0:1])
            t.then_inc(s_row, 1)
            for g in range(G):
                if g in (0, G // 4 // 2 * 4):
                    pe.wait_ge(s_exp, 2 if g else 1)
                t = pe.transpose(bank[g // 4][:, g % 4 * P:(g % 4 + 1) * P], scan[0][:, g * P:(g + 1) * P], ident[:, :])
                if g % 4 == 3:
                    t.then_inc(s_bp, 1)

            pe.wait_ge(s_bc, G // 4)
            with pe.Fori(0, NK // RU) as i:
                for v in range(RU):
                    k = RU * i + v
                    pe.wait_ge(s_oha if v % 2 else s_oh, RU // 2 * i + v // 2 + 1)
                    pe.wait_ge(s_msg, k + UN + 1)
                    pe.wait_ge(s_exc, k + 1)
                    pe.wait_ge(s_acc, k + 1)
                    pe.sem_inc(s_gate_pe, 1)
                    for j in range(2):
                        t = mm(bank[v][:, 0:ROW], hot[:, v, j, 0:P], msg[:, v, j, :], start=j == 0, stop=j == 1)
                    t.then_inc(s_agg, 1)

            pe.wait_ge(s_acc, RU + NK)
            pe.wait_ge(s_wt2, 16 * (1 + 2 * NE + 4))

            def group(g, tiles):
                pe.wait_ge(s_xn2, g + 1)
                pe.sem_inc(s_gate_pe, 1)
                for q in range(tiles):
                    for kb in range(2):
                        t = pe.transpose(bank[kb][:, q * P:(q + 1) * P], xn2[:, q, kb * P:(kb + 1) * P], ident[:, :])
                t.then_inc(s_t2, 1)
                pe.wait_ge(s_xT2, g + 1)
                pe.sem_inc(s_gate_pe, 1)
                for kb in range(2):
                    t = mm(bank[2][:, 0:tiles * P], rw1[:, kb, :], xT_g[:, kb, 0:tiles * P], start=kb == 0, stop=kb == 1)
                t.then_inc(s_rps, 1)
                pe.wait_ge(s_rh, g + 1)
                pe.sem_inc(s_gate_pe, 1)
                for q in range(tiles):
                    t = mm(bank[7][:, ds((g * GW + q) * H, NE)], rh[:, q * P:(q + 1) * P], rw2[:, :], start=True, stop=True)
                t.then_inc(s_lps, 1)

            def rank(part, n):
                pe.wait_ge(s_pick, part + 1)
                m = n * H
                mm(bank[5][:, 0:m], before[:, :], picks[:, 0:m], start=True, stop=True)
                mm(bank[4][:, 0:m], ones[:, :], picks[:, 0:m], start=True, stop=True).then_inc(s_rank, 1)
            picks = places[:, :, :].rearrange("p w h -> p (w h)")
            with pe.Fori(0, PA // GW) as g:
                group(g, GW)
            rank(0, PA)
            with pe.Fori(PA // GW, NG) as g:
                group(g, GW)
            group(NG, 1)
            rank(1, NW - PA)

            pe.wait_ge(s_place, 2)

            def turn(t, u, v, it):
                pe.wait_ge(s_tile[u], 16 * TILE_DMAS * it + 16 * TILE_DMAS)
                pe.wait_ge(s_xTt, t + 1)
                pe.sem_inc(s_gate_pe, 1)
                for kb in range(2):
                    for j in range(TB):
                        o = pe.transpose(bank[6 + v][:, kb * TW + j * P:kb * TW + (j + 1) * P],
                                         rows_in[:, u * TB + j, H + kb * P:H + (kb + 1) * P], ident[:, :])
                o.then_inc(s_Tt, 1)

            def layer(n, out, rhs, u, s):
                for m in range(2):
                    for kb in range(2):
                        o = mm(out[:, m * TW:(m + 1) * TW], w_tile[:, u * 3 + n, kb, m * P:(m + 1) * P],
                               rhs[:, kb * TW:(kb + 1) * TW], start=kb == 0, stop=kb == 1)
                o.then_inc(s, 1)

            def layer1(t, u, v):
                pe.wait_ge(s_xTt, t + 3)
                pe.wait_ge(s_h1, t + 1)
                pe.sem_inc(s_gate_pe, 1)
                layer(0, bank[v], xT2[:, v, :], u, s_l1)

            def layer2(t, u, v):
                pe.wait_ge(s_h1, t + 3)
                pe.wait_ge(s_h2, t + 1)
                pe.sem_inc(s_gate_pe, 1)
                layer(1, bank[2 + v], hT1[:, v, :], u, s_l2)

            def layer3(t, u, v):
                pe.wait_ge(s_h2, t + 3)
                pe.wait_ge(s_y, t + 3)
                pe.sem_inc(s_gate_pe, 1)
                for j in range(TB):
                    for kb in range(2):
                        o = mm(bank[4 + v][:, j * C:(j + 1) * C], hT2[:, v, kb * TW + j * P:kb * TW + (j + 1) * P],
                               w_tile[:, u * 3 + 2, kb, :], start=kb == 0, stop=kb == 1)
                o.then_inc(s_l3, 1)

            def tiles(i, n):
                for u in range(n):
                    t = UT * i + u
                    layer2(t, u, u % 2)
                    turn(t + 2, (u + 2) % UT, u % 2, i + (u + 2) // UT)
                    layer1(t + 1, (u + 1) % UT, (u + 1) % 2)
                    layer3(t, u, u % 2)
            turn(0, 0, 0, 0)
            turn(1, 1, 1, 0)
            layer1(0, 0, 0)
            with pe.Fori(0, NT // UT) as i:
                tiles(i, UT)
            tiles(NT // UT, NT % UT)

        @block.vector
        def _(dve):
            done = [0]

            def link(ins):
                done[0] += 1
                ins.then_inc(s_dve, 1)
                dve.wait_ge(s_dve, done[0])
                return ins

            for s, depth in ((s_hot, 2), (s_prod, 2), (s_al, UN), (s_split, 8), (s_msg, UN), (s_acc, RU), (s_y, UT)):
                dve.sem_inc(s, depth)
            link(dve.memset(we_rows[:, :, :], 0.0))
            link(dve.memset(renc[:, :, :, :, :], 1.0))

            dve.wait_ge(s_const, 9)
            dve.wait_ge(s_wt, 80)
            for q in range(4):
                for half in range(2):
                    c = 4 * half + q
                    link(dve.memset(head_mask[q * D:(q + 1) * D, half, c:c + 1], 1.0))
            for ob in range(2):
                for s in range(2):
                    t = link(dve.tensor_scalar(a_blk[:, ob, s, :], head_mask[:, ob, :], a_col[:, ob, s:s + 1], None, ALU.mult))
            dve.sem_inc(s_ablk, 1)
            link(dve.tensor_copy(we_bf[:, 0, :, :], we[:, :, :]))
            link(dve.tensor_tensor(we_res[:, :, :], we[:, :, :], we_bf[:, 0, :, :], ALU.subtract))
            link(dve.tensor_copy(we_bf[:, 1, :, :], we_res[:, :, :]))
            link(dve.tensor_tensor(we_bf[:, 2, :, :], we_res[:, :, :], we_bf[:, 1, :, :], ALU.subtract))
            for q in range(NPROD):
                link(dve.tensor_copy(we_rows[:, :, q * EF:(q + 1) * EF], we_bf[:, SPLIT_W[q], :, 0:EF]))
            for q in range(3):
                link(dve.tensor_copy(we_rows[:, :, NPROD * EF + q:NPROD * EF + q + 1], we_bf[:, q, :, EF:EF + 1]))
            dve.sem_inc(s_we, 1)

            dve.wait_ge(s_edges, 16 * 11)
            link(dve.tensor_scalar(last_w, dst_i[:, :, EB - 1], WSHIFT, None, ALU.logical_shift_right))
            link(dve.tensor_scalar(prev_w, prev_i, WSHIFT, None, ALU.logical_shift_right))
            link(dve.tensor_tensor(last_k, last_w, block_no[:, :], ALU.add))
            link(dve.tensor_tensor(prev_k, prev_w, block_no[:, :], ALU.add))
            link(dve.tensor_scalar(prev_k, prev_k, -1.0, None, ALU.add))
            for a in range(2):
                link(dve.tensor_scalar(sel_a[:, a, :], iota_free[0:BC, :], prev_k[:, a:a + 1], None, ALU.is_gt))
                link(dve.scalar_tensor_tensor(sel[:, a, :], iota_free[0:BC, :], last_k[:, a:a + 1], sel_a[:, a, :], ALU.is_le, ALU.mult))
                link(dve.tensor_copy(dst_f[:, a, :], dst_i[:, a, :]))
                link(dve.tensor_scalar(dst_f[:, a, :], dst_f[:, a, :], block_no128[:, a:a + 1], None, ALU.add))
                link(dve.tensor_copy(src_f[:, a, :], src_i[:, a, :]))
            dve.sem_inc(s_sel, 1)

            dve.wait_ge(s_selps, 1)
            link(dve.tensor_tensor(window_f[:, :], iota_free[:, :], bank[0][:, 0:NKP], ALU.subtract))
            link(dve.memset(keep[:, :], 0.0))
            link(dve.tensor_tensor(keep[:, 1:NKP], window_f[:, 1:NKP], window_f[:, 0:NKP - 1], ALU.is_equal))
            link(dve.tensor_scalar(window_row[:, :], window_f[0:1, :], float(NW - 1), None, ALU.min))
            dve.wait_ge(s_selps, 2)
            link(dve.tensor_copy(src_col[:, :, :].rearrange("p k j -> p j k"), bank[3][:, 0:2 * NKP].rearrange("p (j k) -> p j k", j=2)))
            dve.sem_inc(s_src, 1)
            dve.wait_ge(s_selps, 3)
            link(dve.scalar_tensor_tensor(drel_col[:, :, :].rearrange("p k j -> p j k"),
                                          iota_free[:, :].unsqueeze(1).broadcast_to([P, 2, NKP]), -float(P),
                                          bank[2][:, 0:2 * NKP].rearrange("p (j k) -> p j k", j=2), ALU.mult, ALU.add))
            dve.wait_ge(s_selps, 4)
            for kb in range(2):
                link(dve.tensor_scalar(drel_bf[:, kb, :], bank[1][0:KC, kb * EB:(kb + 1) * EB], step_no128[:, kb:kb + 1], None, ALU.subtract))
            flat_drel = drel_col[:, :, :].rearrange("p k j -> p (k j)")
            link(dve.tensor_scalar(key[:, :], flat_drel, 0.0, None, ALU.is_ge))
            link(dve.scalar_tensor_tensor(valid[:, :], flat_drel, float(P - 1), key[:, :], ALU.is_le, ALU.mult))
            link(dve.scalar_tensor_tensor(key[:, :].rearrange("p (k j) -> p k j", j=2),
                                          window_f[:, :].unsqueeze(2).broadcast_to([P, NKP, 2]), float(P),
                                          drel_col[:, :, :], ALU.mult, ALU.add))
            link(dve.scalar_tensor_tensor(key[:, :], key[:, :], 1.0, valid[:, :], ALU.add, ALU.mult))
            link(dve.tensor_scalar(key[:, :], key[:, :], -1.0, None, ALU.add))
            link(dve.tensor_copy(head_copies[:, :].rearrange("p (h j) -> p h j", h=H), ident[0:CH, 0:CH].unsqueeze(1).broadcast_to([CH, H, CH])))
            dve.sem_inc(s_key, 1)
            dve.wait_ge(s_selps, 7)
            for c in range(EF):
                link(dve.tensor_copy(ea_r[:, :, c, :], bank[4 + c][0:KC, :].rearrange("p (k e) -> p k e", k=2)))
            for kb in range(2):
                hi, mid, lo = (ea_bf[:, kb * 9 + s * EF:kb * 9 + (s + 1) * EF, :] for s in range(3))
                link(dve.tensor_copy(hi, ea_r[:, kb, :, :]))
                link(dve.tensor_tensor(ea_r[:, kb, :, :], ea_r[:, kb, :, :], hi, ALU.subtract))
                link(dve.tensor_copy(mid, ea_r[:, kb, :, :]))
                link(dve.tensor_tensor(lo, ea_r[:, kb, :, :], mid, ALU.subtract))
            dve.sem_inc(s_logsrc, 1)

            def first_norm():
                with dve.Fori(0, NW // 5) as i:
                    for q in range(5):
                        dve.bn_stats(flat(stats[:, ds(5 * i + q, 1), :]), flat(xs[:, ds(5 * i + q, 1), :])).then_inc(s_bn, 1)
                dve.wait_ge(s_bn, NW)
                link(dve.tensor_tensor(mean[:, :], stats[:, :, 1], stats[:, :, 4], ALU.add))
                link(dve.tensor_scalar(mean[:, :], mean[:, :], 0.5, None, ALU.mult))
                link(dve.tensor_tensor(lt[:, 1, :], stats[:, :, 1], stats[:, :, 4], ALU.subtract))
                link(dve.tensor_tensor(lt[:, 1, :], lt[:, 1, :], lt[:, 1, :], ALU.mult))
                link(dve.tensor_tensor(lt[:, 2, :], stats[:, :, 2], stats[:, :, 5], ALU.add))
                link(dve.tensor_scalar(lt[:, 2, :], lt[:, 2, :], 1.0 / C, EPS, ALU.mult, ALU.add))
                link(dve.scalar_tensor_tensor(lt[:, 0, :], lt[:, 1, :], 0.25, lt[:, 2, :], ALU.mult, ALU.add))
                dve.sem_inc(s_var, 1)
                dve.wait_ge(s_std, 1)
                link(dve.reciprocal(rstd[:, :], rstd[:, :]))

            def normalise(w, slot, freed, made):
                dve.wait_ge(freed, w + 1)
                dve.tensor_scalar(xn[:, slot, :], flat(xs[:, ds(w, 1), :]), mean[:, ds(w, 1)], rstd[:, ds(w, 1)],
                                  ALU.subtract, ALU.mult).then_inc(made, 1)

            dve.wait_ge(s_x, 32)
            dve.wait_ge(s_pad, 5)
            first_norm()
            normalise(0, 0, s_xnT, s_xn)
            normalise(1, 1, s_xnT, s_xn)

            def split(i, slot, q, lap):
                w = 2 * i + slot
                if inside(w + 2):
                    normalise(w + 2, slot, s_xnT, s_xn)
                dve.wait_ge(s_hf, w + 3)
                dve.sem_inc(s_gate_dve, 1)
                hi, mid, lo = (h_parts[:, ds(w, 1), s, :].rearrange("p a c -> p (a c)") for s in range(3))
                dve.tensor_copy(hi, hf[:, q, H:HALL]).then_inc(s_split, 1)
                dve.wait_ge(s_split, 4 * w + 9)
                dve.tensor_tensor(hr[:, :], hf[:, q, H:HALL], hi, ALU.subtract).then_inc(s_split, 1)
                dve.wait_ge(s_split, 4 * w + 10)
                dve.sem_inc(s_gate_dve, 1)
                dve.tensor_copy(mid, hr[:, :]).then_inc(s_split, 1)
                dve.wait_ge(s_split, 4 * w + 11)
                dve.tensor_tensor(lo, hr[:, :], mid, ALU.subtract).then_inc(s_split, 1)
            windows(dve, split)

            dve.wait_ge(s_keyT, G // 4)
            dve.wait_ge(s_logs, 16 * 2 * (1 + NPROD))
            link(dve.tensor_tensor(resets[:, 1:SL], key_T[:, 1:SL], key_T[:, 0:SL - 1], ALU.not_equal))
            link(dve.memset(resets[:, 0:1], 0.0))
            link(dve.memset(resets[:, SL:SL + 1], 0.0))
            link(dve.tensor_scalar(resets, resets, -BIG, None, ALU.mult))
            link(dve.tensor_copy(ends[:, 2:3], key_T[:, 0:1]))
            link(dve.tensor_copy(ends[:, 3:4], key_T[:, SL - 1:SL]))
            link(dve.memset(alpha[:, :, 2 * NK:NSUB], 0.0))

            def one_hot(k, u, kp):
                dve.wait_ge(s_drel[u // 2], 16 * kp + 16)
                dve.wait_ge(s_hd, k)
                dve.tensor_scalar(hotT[:, u, :], drel_b[:, u // 2, u % 2, :], iota_part[:, 0:1], None, ALU.is_equal).then_inc(s_hot, 1)

            def products(k, v):
                dve.wait_ge(s_relu, k + 3)
                dve.wait_ge(s_hd, k + 4)
                dve.tensor_tensor(prod[:, v, :, :, 0:D1], renc[:, v, :, :, :],
                                  banks[:, 2 * v:2 * v + 2, 0:CA].rearrange("p j (h d) -> p j h d", h=H), ALU.mult).then_inc(s_prod, 1)

            def add_heads(k, v):
                dve.wait_ge(s_prod, k + 3)
                dve.wait_ge(s_as, k + 1)
                dve.sem_inc(s_gate_dve, 1)
                dve.tensor_reduce(sums[:, v, :, :], prod[:, v, :, :, :], AX.X, ALU.add).then_inc(s_sum, 1)

            def leak(k, v):
                dve.wait_ge(s_sum, k + 1)
                dve.scalar_tensor_tensor(slots[:, ds(2 * k, 2), :], sums[:, v, :, :], 0.2, sums[:, v, :, :],
                                         ALU.mult, ALU.max).then_inc(s_al, 1)

            dve.wait_ge(s_drel[0], 16)
            dve.tensor_scalar(hotT[:, 0, :], drel_b[:, 0, 0, :], iota_part[:, 0:1], None, ALU.is_equal).then_inc(s_hot, 1)
            one_hot(1, 1, 0)
            with dve.Fori(0, NK // 4) as i:
                for u in range(4):
                    k = 4 * i + u
                    products(k, u % 2)
                    one_hot(k + 2, (u + 2) % 4, i + (u + 2) // 4)
                    add_heads(k, u % 2)
                    leak(k, u % 2)

            dve.wait_ge(s_tc, G // 4)
            logit_T = scan[2]
            link(dve.tensor_tensor_scan(scan[0], resets[:, 0:SL], logit_T, -BIG, ALU.add, ALU.max))
            link(dve.tensor_tensor_scan(scan[3][:, ::-1], resets[:, 1:SL + 1][:, ::-1], scan[0][:, ::-1], -BIG, ALU.add, ALU.max))
            link(dve.tensor_copy(ends[:, 0:1], scan[0][:, SL - 1:SL]))
            link(dve.tensor_copy(ends[:, 1:2], scan[3][:, 0:1]))
            dve.sem_inc(s_ends, 1)

            dve.wait_ge(s_row, 1)
            link(dve.tensor_copy(erow[:, :, :].rearrange("p a n -> p (a n)"), bank[0][0:1, :]))
            last_max, first_max, first_key, last_key = (erow[:, c, :] for c in range(4))
            broken, cut, step_f, run_f, step_b, run_b = (dlink[:, c, :] for c in range(6))
            link(dve.tensor_tensor(broken, first_key, last_key, ALU.not_equal))
            link(dve.tensor_scalar(broken, broken, -BIG, None, ALU.mult))
            link(dve.tensor_tensor(cut[:, 1:P], first_key[:, 1:P], last_key[:, 0:P - 1], ALU.not_equal))
            link(dve.memset(cut.rearrange("p (h j) -> p h j", h=H)[:, :, 0], 1.0))
            link(dve.tensor_scalar(cut, cut, -BIG, None, ALU.mult))
            link(dve.tensor_tensor(step_f, cut, broken, ALU.add))
            link(dve.memset(step_b, -BIG))
            link(dve.tensor_tensor(step_b[:, 0:P - 1], cut[:, 1:P], broken[:, 0:P - 1], ALU.add))
            link(dve.tensor_tensor_scan(run_f, step_f, last_max, -BIG, ALU.add, ALU.max))
            link(dve.tensor_tensor_scan(run_b[:, ::-1], step_b[:, ::-1], first_max[:, ::-1], -BIG, ALU.add, ALU.max))
            link(dve.memset(carry[:, :, :], -BIG))
            link(dve.tensor_tensor(carry[:, 0, 1:P], run_f[:, 0:P - 1], cut[:, 1:P], ALU.add))
            link(dve.tensor_tensor(carry[:, 1, 0:P - 1], run_b[:, 1:P], cut[:, 1:P], ALU.add))
            dve.sem_inc(s_carry, 1)
            dve.wait_ge(s_row, 2)
            link(dve.tensor_copy(carry_c[:, :], bank[1][:, 0:2]))
            link(dve.tensor_tensor_scan(scan[0], resets[:, 0:SL], logit_T, carry_c[:, 0:1], ALU.add, ALU.max))
            link(dve.tensor_tensor_scan(scan[3][:, ::-1], resets[:, 1:SL + 1][:, ::-1], scan[0][:, ::-1], carry_c[:, 1:2], ALU.add, ALU.max))
            half = G // 4 // 2 * 4 * P
            for cols in (slice(0, half), slice(half, SL)):
                link(dve.tensor_tensor(logit_T[:, cols], logit_T[:, cols], scan[3][:, cols], ALU.subtract))
                dve.sem_inc(s_dif, 1)

            dve.wait_ge(s_hd, 3 + NK)
            link(dve.memset(lg[:, :, NE:H], -1.0))
            link(dve.memset(pad_rows, 0.0))
            link(dve.memset(ones[:, :], 1.0))
            link(dve.memset(keep_w, 1.0))
            link(dve.memset(keep_w[:, :, 0], 0.0))
            link(dve.memset(count_e[:, :], 0.0))
            link(dve.tensor_scalar(before[:, :], iota_free[:, 0:P], iota_part[:, 0:1], None, ALU.is_gt))
            for j in range(TB):
                link(dve.tensor_scalar(pad_rows[:, j, NODE_COL:H], iota_part[:, 0:1], float(NODES + j * P), None, ALU.add))
            link(dve.tensor_scalar(node_no[:, :], iota_free[:, 0:NW], float(P), iota_part[:, 0:1], ALU.mult, ALU.add))
            link(dve.tensor_scalar(is_node[:, :], node_no[:, :], float(NODES), None, ALU.is_lt))
            for c in range(TOPK):
                link(dve.tensor_scalar(dump_row[:, c, :], is_node[:, :], -1.0, 1.0, ALU.mult, ALU.add))
                link(dve.tensor_scalar(place_c, is_node[:, :], 0.0, iota_part[:, 0:1], ALU.mult, ALU.add))
                link(dve.tensor_scalar(place_c, place_c, float(DUMP + c * P), None, ALU.add))
                link(dve.tensor_tensor(dump_row[:, c, :], dump_row[:, c, :], place_c, ALU.mult))
            link(dve.memset(sums_to, 0.0))

            link(dve.memset(run[:, RU - 1, :], 0.0))
            dve.wait_ge(s_bc, G // 4)

            def weigh(k, u, i):
                dve.wait_ge(s_ld[u], 16 * i + 16)
                dve.wait_ge(s_agg, k + 1)
                dve.tensor_tensor(msg[:, u % RU, :, H:ROW].rearrange("p j (h d) -> p j h d", h=H),
                                  gath[:, u, :, H:HALL].rearrange("p j (h d) -> p j h d", h=H)[:, :, :, 0:D],
                                  slots[:, ds(2 * k, 2), :].unsqueeze(3).broadcast_to([P, 2, H, D]), ALU.mult).then_inc(s_msg, 1)

            def spread(k, v):
                dve.wait_ge(s_agg, k + 1)
                dve.tensor_tensor(hot[:, v, :, 0:P], iota_free[:, 0:P].unsqueeze(1).broadcast_to([P, 2, P]),
                                  flat(drel_col[:, ds(k, 1), :]).unsqueeze(2).broadcast_to([P, 2, P]),
                                  ALU.is_equal).then_inc(s_oh, 1)

            def add_up(k, v, half):
                dve.wait_ge(s_agg, k + RU + 1)
                dve.wait_ge(s_acc, k + RU)
                dve.wait_ge(s_puta if v % 2 else s_put, half + 1)
                dve.scalar_tensor_tensor(run[:, v, :], run[:, (v - 1) % RU, :], keep[:, ds(k, 1)], bank[v][:, 0:ROW],
                                         ALU.mult, ALU.add).then_inc(s_acc, 1)

            def second_phase(i, n, peeled=False):
                for u in range(n):
                    k = UN * i + u
                    if u % 2 == 0:
                        spread(k, u % RU)
                    weigh(k, u, i)
                    if not (peeled and u < LAG):
                        add_up(k - LAG, (u - LAG) % RU, UN // 2 * i + (u - LAG) // 2)
            second_phase(0, UN, peeled=True)
            with dve.Fori(1, NI) as i:
                second_phase(i, UN)
            second_phase(NI, REST)
            for k in range(NK - LAG, NK):
                add_up(k, k % RU, k // 2)

            dve.wait_ge(s_acc, RU + NK)
            dve.wait_ge(s_put, 2 + NK // 2)
            dve.wait_ge(s_puta, 2 + NK // 2)
            dve.wait_ge(s_wt2, 16 * (1 + 2 * NE + 4))
            step = [0, 0]

            def next_link(g, ins):
                step[0] += 1
                ins.then_inc(s_prep, 1)
                dve.wait_ge(s_prep, g * step[1] + step[0])

            def finish(g, tiles):
                step[0] = 0
                a = acc[:, ds(g * GW, tiles), :]
                heads = a[:, :, H:ROW].rearrange("p w (h d) -> p w h d", h=H)
                x_g = xs[:, ds(g * GW, tiles), :]
                den, st = rden[:, 0:tiles, :], stats[:, 0:tiles, :]
                mean_g, rstd_g = mean[:, 0:tiles], rstd[:, 0:tiles]
                lt_g = [lt[:, c, 0:tiles] for c in range(3)]
                next_link(g, dve.tensor_scalar(den, a[:, :, 0:H], 1e-10, None, ALU.max))
                next_link(g, dve.reciprocal(den, den))
                next_link(g, dve.tensor_tensor(heads, heads, den.unsqueeze(3).broadcast_to([P, tiles, H, D]), ALU.mult))
                next_link(g, dve.tensor_tensor(x_g, x_g, a[:, :, H:ROW], ALU.add))
                dve.sem_inc(s_gate_dve, 1)
                for q in range(tiles):
                    b = dve.bn_stats(stats[:, q, :], flat(xs[:, ds(g * GW + q, 1), :]))
                next_link(g, b)
                next_link(g, dve.tensor_tensor(mean_g, st[:, :, 1], st[:, :, 4], ALU.add))
                next_link(g, dve.tensor_scalar(mean_g, mean_g, 0.5, None, ALU.mult))
                next_link(g, dve.tensor_tensor(lt_g[1], st[:, :, 1], st[:, :, 4], ALU.subtract))
                next_link(g, dve.tensor_tensor(lt_g[1], lt_g[1], lt_g[1], ALU.mult))
                next_link(g, dve.tensor_tensor(lt_g[2], st[:, :, 2], st[:, :, 5], ALU.add))
                next_link(g, dve.tensor_scalar(lt_g[2], lt_g[2], 1.0 / C, EPS, ALU.mult, ALU.add))
                next_link(g, dve.scalar_tensor_tensor(lt_g[0], lt_g[1], 0.25, lt_g[2], ALU.mult, ALU.add))
                dve.sem_inc(s_var, 1)
                dve.wait_ge(s_std, g + 2)
                next_link(g, dve.reciprocal(rstd_g, rstd_g))
                dve.wait_ge(s_t2, g + 1)
                dve.wait_ge(s_xkeep, g + 1)
                for q in range(tiles):
                    n = dve.tensor_scalar(xn2[:, q, :], flat(xs[:, ds(g * GW + q, 1), :]), mean[:, q:q + 1], rstd[:, q:q + 1],
                                          ALU.subtract, ALU.mult)
                n.then_inc(s_xn2, 1)

            def choose(part, w0, n, groups):
                def over(ap, m):
                    return ap.unsqueeze(2).broadcast_to([P, n, m])
                ws = slice(w0, w0 + n)
                l_g, r_g = lg[:, ws, 0:NE], [rsm[:, c, ws] for c in range(6)]
                p1, p2 = pick1[:, ws, :], pick2[:, ws, :]
                dve.wait_ge(s_lps, groups)
                link(dve.tensor_tensor(l_g, bank[7][:, w0 * H:(w0 + n) * H].rearrange("p (w h) -> p w h", w=n)[:, :, 0:NE],
                                       rb2_b[:, :].unsqueeze(1).broadcast_to([P, n, NE]), ALU.add))
                link(dve.tensor_reduce(r_g[0], l_g, AX.X, ALU.max))
                link(dve.tensor_tensor(l_g, l_g, over(r_g[0], NE), ALU.subtract))
                dve.sem_inc(s_soft, 1)
                dve.wait_ge(s_softe, part + 1)
                link(dve.tensor_reduce(r_g[0], l_g, AX.X, ALU.add))
                link(dve.reciprocal(r_g[0], r_g[0]))
                link(dve.tensor_tensor(l_g, l_g, over(r_g[0], NE), ALU.mult))
                for w in range(w0, w0 + n):
                    m = dve.max(top[:, w, :], lg[:, w, :])
                link(m)
                for w in range(w0, w0 + n):
                    m = dve.max_index(topi[:, w, :], top[:, w, :], lg[:, w, :])
                link(m)
                link(dve.tensor_tensor(r_g[1], top[:, ws, 1], top[:, ws, 0], ALU.subtract))
                dve.sem_inc(s_gap, 1)
                link(dve.tensor_copy(topf[:, ws, :], topi[:, ws, 0:2]))
                nos = iota_free[:, 0:H].unsqueeze(1).broadcast_to([P, n, H])
                link(dve.tensor_tensor(p1, nos, over(topf[:, ws, 0], H), ALU.is_equal))
                link(dve.tensor_tensor(p2, nos, over(topf[:, ws, 1], H), ALU.is_equal))
                m_all = places[:, 0:n, :]
                link(dve.tensor_tensor(m_all, p1, p2, ALU.add))
                link(dve.tensor_tensor(m_all, m_all, over(is_node[:, ws], H), ALU.mult))
                dve.sem_inc(s_pick, 1)
                dve.wait_ge(s_gape, part + 1)
                link(dve.tensor_scalar(r_g[3], r_g[2], 1.0, None, ALU.add))
                link(dve.reciprocal(r_g[3], r_g[3]))
                link(dve.tensor_tensor(r_g[4], r_g[2], r_g[3], ALU.mult))
                a_w = acc[:, ws, 0:H]
                wt2 = top[:, ws, :]
                link(dve.tensor_tensor(a_w, p1, over(r_g[3], H), ALU.mult))
                link(dve.tensor_tensor(wt2, p2, over(r_g[4], H), ALU.mult))
                link(dve.tensor_tensor(a_w, a_w, wt2, ALU.add))
                link(dve.tensor_copy(acc[:, ws, NODE_COL], node_no[:, ws]))
                dve.wait_ge(s_rank, part + 1)
                tot, inc = totals[:, :, 0:n], sums_to[:, :, 0:n]
                link(dve.tensor_copy(tot, bank[4][:, 0:n * H].rearrange("p (w h) -> p h w", w=n)))
                for e in range(NE):
                    last = dve.tensor_tensor_scan(inc[:, e, :], keep_w[:, e, 0:n], tot[:, e, :], 0.0, ALU.mult, ALU.add)
                link(last)
                link(dve.tensor_tensor(tot, inc, tot, ALU.subtract))
                link(dve.tensor_tensor(tot, tot, count_e[:, :].unsqueeze(2).broadcast_to([P, H, n]), ALU.add))
                link(dve.tensor_tensor(count_e[:, 0:NE], count_e[:, 0:NE], inc[:, 0:NE, n - 1], ALU.add))
                link(dve.tensor_tensor(m_all, bank[5][:, 0:n * H].rearrange("p (w h) -> p w h", w=n), tot.rearrange("p h w -> p w h"), ALU.add))
                link(dve.scalar_tensor_tensor(m_all, nos, float(RX), m_all, ALU.mult, ALU.add))
                for c, pick in enumerate((p1, p2)):
                    link(dve.tensor_tensor(wt2, pick, m_all, ALU.mult))
                    link(dve.tensor_reduce(place_c[:, ws], wt2, AX.X, ALU.add))
                    link(dve.tensor_tensor(place_c[:, ws], place_c[:, ws], is_node[:, ws], ALU.mult))
                    link(dve.tensor_tensor(place[:, ws, c], place_c[:, ws], dump_row[:, c, ws], ALU.add))
                dve.sem_inc(s_place, 1)

            dve.wait_ge(s_biased, 1)
            finish(0, GW)
            step[1] = step[0]
            with dve.Fori(1, PA // GW) as g:
                finish(g, GW)
            choose(0, 0, PA, PA // GW)
            with dve.Fori(PA // GW, NG) as g:
                finish(g, GW)
            finish(NG, 1)
            choose(1, PA, NW - PA, NG + 1)

            n_e, tiles_e, upto = (tile_f[:, c, 0:NE] for c in range(3))
            nos_e = iota_free[0:1, 0:NE]
            link(dve.tensor_scalar(tiles_i[:, 0:NE], count_e[0:1, 0:NE], float(TW - 1), None, ALU.add))
            link(dve.tensor_scalar(tiles_i[:, 0:NE], tiles_i[:, 0:NE], TWSHIFT, None, ALU.logical_shift_right))
            link(dve.tensor_copy(tiles_e, tiles_i[:, 0:NE]))
            link(dve.scalar_tensor_tensor(pad_at[:, 0:NE], nos_e, float(RX), count_e[0:1, 0:NE], ALU.mult, ALU.add))
            link(dve.memset(n_e, 1.0))
            link(dve.tensor_tensor_scan(upto, n_e, tiles_e, 0.0, ALU.mult, ALU.add))
            done_e, done_t = (tile_cmp[:, c, :].rearrange("p (t e) -> p t e", e=NE) for c in range(2))
            q_expert, q_before, q_row, q_lim = (tile_q[:, c, :] for c in range(4))
            tile_no = iota_free[0:1, 0:NTP]
            wide = [1, NTP, NE]
            link(dve.tensor_tensor(done_e, upto.unsqueeze(1).broadcast_to(wide), tile_no.unsqueeze(2).broadcast_to(wide), ALU.is_le))
            link(dve.tensor_tensor(done_t, done_e, tiles_e.unsqueeze(1).broadcast_to(wide), ALU.mult))
            link(dve.tensor_reduce(q_expert, done_e, AX.X, ALU.add))
            link(dve.tensor_reduce(q_before, done_t, AX.X, ALU.add))
            link(dve.tensor_tensor(q_row, tile_no, q_before, ALU.subtract))
            link(dve.tensor_scalar(q_row, q_row, float(TW), None, ALU.mult))
            link(dve.scalar_tensor_tensor(q_row, q_expert, float(RX), q_row, ALU.mult, ALU.add))
            link(dve.tensor_scalar(tile_row[:, :], q_row, float(SPARE), None, ALU.min))
            link(dve.tensor_scalar(tile_expert[:, :], q_expert, float(NE - 1), None, ALU.min))
            dve.sem_inc(s_table, 1)

            def weigh_tile(t, u, v):
                e = dve.value_load(tile_expert[0:1, ds(t, 1)], min_val=0, max_val=NE - 1)
                dve.wait_ge(s_l3, t + 3)
                dve.wait_ge(s_added, t + 1)
                y = y_out[:, v * TB:(v + 1) * TB, :]
                rows = rows_in[:, u * TB:(u + 1) * TB, :]
                dve.tensor_tensor(y, bank[4 + v].rearrange("p (j c) -> p j c", j=TB),
                                  b3_tile[:, u, :].unsqueeze(1).broadcast_to([P, TB, C]), ALU.add).then_inc(s_yb, 1)
                dve.sem_inc(s_gate_dve, 1)
                dve.tensor_copy(node_idx[:, v, :], rows[:, :, NODE_COL])
                dve.wait_ge(s_yb, t + 1)
                for j in range(TB):
                    o = dve.tensor_scalar(y[:, j, :], y[:, j, :], rows[:, j, ds(e, 1)], None, ALU.mult)
                o.then_inc(s_y, 1)

            def tiles(i, n):
                for u in range(n):
                    weigh_tile(UT * i + u, u, u % 2)
            with dve.Fori(0, NT // UT) as i:
                tiles(i, UT)
            tiles(NT // UT, NT % UT)


_INS = ["x", "src", "dst", "edge_attr_3", "L0_gnn_W", "L0_gnn_a_src", "L0_gnn_a_dst", "L0_gnn_edge_W",
        "L0_gnn_edge_b", "L0_gnn_bias", "L0_ffn_router_w1", "L0_ffn_router_b1", "L0_ffn_router_w2",
        "L0_ffn_router_b2", "L0_ffn_expert_w1", "L0_ffn_expert_b1", "L0_ffn_expert_w2", "L0_ffn_expert_b2",
        "L0_ffn_expert_w3", "L0_ffn_expert_b3"]


def kernel(**inputs):
    import numpy as _np
    import concourse.bacc as _bacc
    from concourse import mybir as _mybir
    from concourse.bass_utils import run_bass_kernel_spmd as _run

    nc = _bacc.Bacc("TRN2", target_bir_lowering=False, num_devices=1)
    arrays, args = {}, []
    for name in _INS:
        a = _np.ascontiguousarray(inputs[name])
        arrays[f"in_{name}_dram"] = a
        args.append(nc.dram_tensor(f"in_{name}_dram", a.shape, _mybir.dt.from_np(a.dtype), kind="ExternalInput").ap())
    args.append(nc.dram_tensor("out_0_dram", (NODES, C), _mybir.dt.float32, kind="ExternalOutput").ap())
    bass_gnn_moe(nc, *args)
    r = _run(nc, [arrays], core_ids=[0])
    return r.results[0]["out_0_dram"]
```
